# Optimizing a Trainium2 kernel written in Bass

```python
import numpy as np
import jax
import jax.numpy as jnp

def _softmax(x, axis=-1):
    return jax.nn.softmax(x, axis=axis)

def _gelu(x):
    return jax.nn.gelu(x, approximate=True)

def _silu(x):
    return jax.nn.silu(x)

def _sigmoid(x):
    return jax.nn.sigmoid(x)

def _layernorm(x, axis=-1, eps=1e-05):
    m = jnp.mean(x, axis=axis, keepdims=True)
    v = jnp.var(x, axis=axis, keepdims=True)
    return (x - m) / jnp.sqrt(v + eps)

def _scatter_add(tgt, idx, src, axis=0):
    return tgt.at[idx].add(src)

def _segment_sum(src, seg, n):
    return jax.ops.segment_sum(src, seg, n)
kernel_name = 'mk_macaron_d1_jaxref_r8_adf06d'

def setup_inputs(seed: int=0):
    np.random.seed(seed)
    _w = jnp.asarray

    def _L0_attn_setup():
        import jax, jax.numpy as jnp
        import numpy as np
        HIDDEN = 256
        NUM_HEADS = 16
        NUM_KV_HEADS = 4
        HEAD_DIM = 128
        ROPE_BASE = 10000.0

        def apply_rope(x):
            B, H, S, D = x.shape
            half = D // 2
            inv_freq = 1.0 / ROPE_BASE ** (jnp.arange(half, dtype=jnp.float32) / half)
            ang = jnp.arange(S, dtype=jnp.float32)[:, None] * inv_freq[None, :]
            cos = jnp.cos(ang).astype(x.dtype)
            sin = jnp.sin(ang).astype(x.dtype)
            x1, x2 = (x[..., :half], x[..., half:])
            return jnp.concatenate([x1 * cos - x2 * sin, x1 * sin + x2 * cos], axis=-1)
        key = jax.random.key(seed)
        ks = jax.random.split(key, 6)
        B, S = (2, 256)
        sd = 1.0 / np.sqrt(HIDDEN)
        x = jax.random.normal(ks[0], (B, S, HIDDEN), dtype=jnp.float32)
        wq = jax.random.normal(ks[1], (NUM_HEADS * HEAD_DIM, HIDDEN), dtype=jnp.float32) * sd
        wk = jax.random.normal(ks[2], (NUM_KV_HEADS * HEAD_DIM, HIDDEN), dtype=jnp.float32) * sd
        wv = jax.random.normal(ks[3], (NUM_KV_HEADS * HEAD_DIM, HIDDEN), dtype=jnp.float32) * sd
        wo = jax.random.normal(ks[4], (HIDDEN, NUM_HEADS * HEAD_DIM), dtype=jnp.float32) * sd
        key_weights = jnp.ones((NUM_HEADS,), dtype=jnp.float32)
        return {'x': x, 'wq': wq, 'wk': wk, 'wv': wv, 'wo': wo, 'key_weights': key_weights}
    _L0_attn_in = _L0_attn_setup()

    def _L0_ffn_setup():
        import jax, jax.numpy as jnp
        import numpy as np
        TOP_K = 2
        EPS = 1e-06
        key = jax.random.key(seed)
        ks = jax.random.split(key, 5)
        B, S, D, E = (4, 256, 256, 8)
        sd = 1.0 / np.sqrt(D)
        return {'x': jax.random.normal(ks[0], (B, S, D), jnp.float32), 'router_w': jax.random.normal(ks[1], (D, E), jnp.float32) * sd, 'router_b': jnp.zeros((E,), jnp.float32), 'expert_w': jax.random.normal(ks[2], (E, D, D), jnp.float32) * sd, 'expert_b': jnp.zeros((E, D), jnp.float32), 'proj_w': jax.random.normal(ks[3], (D, D), jnp.float32) * sd, 'proj_b': jnp.zeros((D,), jnp.float32), 'norm_w': jnp.ones((D,), jnp.float32)}
    _L0_ffn_in = _L0_ffn_setup()
    _d = {'L0_attn_x': _L0_attn_in['x'], 'L0_attn_wq': _L0_attn_in['wq'], 'L0_attn_wk': _L0_attn_in['wk'], 'L0_attn_wv': _L0_attn_in['wv'], 'L0_attn_wo': _L0_attn_in['wo'], 'L0_attn_key_weights': _L0_attn_in['key_weights'], 'L0_ffn_router_w': _L0_ffn_in['router_w'], 'L0_ffn_router_b': _L0_ffn_in['router_b'], 'L0_ffn_expert_w': _L0_ffn_in['expert_w'], 'L0_ffn_expert_b': _L0_ffn_in['expert_b'], 'L0_ffn_proj_w': _L0_ffn_in['proj_w'], 'L0_ffn_proj_b': _L0_ffn_in['proj_b'], 'L0_ffn_norm_w': _L0_ffn_in['norm_w']}
    _x0 = _d['L0_attn_x']
    _d['L0_attn_x'] = jax.random.normal(jax.random.fold_in(jax.random.key(seed), 1), (4, 512, 256), dtype=_x0.dtype)
    del _x0
    return _d

def reference(L0_attn_x, L0_attn_wq, L0_attn_wk, L0_attn_wv, L0_attn_wo, L0_attn_key_weights, L0_ffn_router_w, L0_ffn_router_b, L0_ffn_expert_w, L0_ffn_expert_b, L0_ffn_proj_w, L0_ffn_proj_b, L0_ffn_norm_w):

    def _L0_attn_ref(x, wq, wk, wv, wo, key_weights):
        import jax, jax.numpy as jnp
        import numpy as np
        HIDDEN = 256
        NUM_HEADS = 16
        NUM_KV_HEADS = 4
        HEAD_DIM = 128
        ROPE_BASE = 10000.0

        def apply_rope(x):
            B, H, S, D = x.shape
            half = D // 2
            inv_freq = 1.0 / ROPE_BASE ** (jnp.arange(half, dtype=jnp.float32) / half)
            ang = jnp.arange(S, dtype=jnp.float32)[:, None] * inv_freq[None, :]
            cos = jnp.cos(ang).astype(x.dtype)
            sin = jnp.sin(ang).astype(x.dtype)
            x1, x2 = (x[..., :half], x[..., half:])
            return jnp.concatenate([x1 * cos - x2 * sin, x1 * sin + x2 * cos], axis=-1)
        B, S, _ = x.shape
        g = NUM_HEADS // NUM_KV_HEADS
        scale = HEAD_DIM ** (-0.5)
        q = (x @ wq.T).reshape(B, S, NUM_HEADS, HEAD_DIM).transpose(0, 2, 1, 3)
        k = (x @ wk.T).reshape(B, S, NUM_KV_HEADS, HEAD_DIM).transpose(0, 2, 1, 3)
        v = (x @ wv.T).reshape(B, S, NUM_KV_HEADS, HEAD_DIM).transpose(0, 2, 1, 3)
        q = apply_rope(q)
        k = apply_rope(k)
        k = jnp.repeat(k, g, axis=1)
        v = jnp.repeat(v, g, axis=1)
        k = k * key_weights[None, :, None, None]
        scores = jnp.einsum('bhqd,bhkd->bhqk', q, k) * scale
        causal = jnp.triu(jnp.ones((S, S), dtype=bool), k=1)
        scores = jnp.where(causal, -jnp.inf, scores)
        attn = jax.nn.softmax(scores, axis=-1)
        out = jnp.einsum('bhqk,bhkd->bhqd', attn, v)
        out = out.transpose(0, 2, 1, 3).reshape(B, S, NUM_HEADS * HEAD_DIM)
        return out @ wo.T

    def _L0_ffn_ref(x, router_w, router_b, expert_w, expert_b, proj_w, proj_b, norm_w):
        import jax, jax.numpy as jnp
        import numpy as np
        TOP_K = 2
        EPS = 1e-06
        B, S, D = x.shape
        E = router_b.shape[0]
        logits = jnp.einsum('bsd,de->bse', x, router_w) + router_b
        topk_vals, topk_idx = jax.lax.top_k(logits, TOP_K)
        topk_w = jax.nn.softmax(topk_vals, axis=-1)
        full_w = jnp.sum(jax.nn.one_hot(topk_idx, E, dtype=x.dtype) * topk_w[..., None], axis=-2)
        xf = x.reshape(-1, D)
        h = jnp.einsum('td,edf->etf', xf, expert_w) + expert_b[:, None, :]
        expert_out = jax.nn.silu(h)
        combined = jnp.einsum('etf,te->tf', expert_out, full_w.reshape(-1, E)).reshape(B, S, D)
        out = jnp.einsum('bsd,df->bsf', combined, proj_w) + proj_b
        y = x + out
        rms = jnp.sqrt(jnp.mean(y * y, axis=-1, keepdims=True) + EPS)
        return norm_w * (y / rms)
    x = L0_attn_x
    x = x + 0.5 * _L0_ffn_ref(_layernorm(x, axis=-1), L0_ffn_router_w, L0_ffn_router_b, L0_ffn_expert_w, L0_ffn_expert_b, L0_ffn_proj_w, L0_ffn_proj_b, L0_ffn_norm_w)
    x = x + _L0_attn_ref(_layernorm(x, axis=-1), L0_attn_wq, L0_attn_wk, L0_attn_wv, L0_attn_wo, L0_attn_key_weights)
    x = x + 0.5 * _L0_ffn_ref(_layernorm(x, axis=-1), L0_ffn_router_w, L0_ffn_router_b, L0_ffn_expert_w, L0_ffn_expert_b, L0_ffn_proj_w, L0_ffn_proj_b, L0_ffn_norm_w)
    return x

_drawn_inputs = setup_inputs


def setup_inputs(seed=0):
    import zlib

    import numpy as np

    out = dict(_drawn_inputs(seed))
    spreads = {'L0_attn_key_weights': (1.0, 0.2),
     'L0_ffn_router_b': (0.0, 0.1),
     'L0_ffn_expert_b': (0.0, 0.271),
     'L0_ffn_proj_b': (0.0, 0.1),
     'L0_ffn_norm_w': (1.0, 0.2)}
    factors = {}
    for name, (base, spread) in spreads.items():
        noise = np.random.default_rng([zlib.crc32(name.encode()), seed]).standard_normal(out[name].shape)
        drawn = base * np.exp(spread * noise) if base else spread * noise
        out[name] = jnp.asarray(drawn.astype(out[name].dtype))
    for name, factor in factors.items():
        out[name] = (out[name] * factor).astype(out[name].dtype)
    return out
```

```python
from contextlib import ExitStack

import numpy as np

import concourse.bass as bass
from concourse import mybir

F32 = mybir.dt.float32
F32R = mybir.dt.float32r
U32 = mybir.dt.uint32
ALU = mybir.AluOpType
ACT = mybir.ActivationFunctionType

P = 128
D = 256
C = D // P
BATCH, SEQ = 4, 512
TOKENS = BATCH * SEQ
TILES = TOKENS // P
BT = SEQ // P
HEADS, KV, HD = 16, 4, 128
G = HEADS // KV
E = 8
LN_EPS = 1e-5
RMS_EPS = 1e-6
QKV = (G + 2) * HD
GW = C * QKV + G * D
BIG = 1e30
ROPE_BASE = 10000.0


def layer_norm_block(dve, x, j, st, mv, ve, rs, z, ln_stats, ln_aggr, ln_var, rstd_done, z_done, passed):
    for t in range(BT):
        dve.bn_stats(st[:, t, :], x[:, bass.ds(j * BT + t, 1), :]).then_inc(ln_stats, 1)
    dve.wait_ge(ln_stats, j * BT + BT).then_inc(passed, 1)
    for t in range(BT):
        dve.bn_aggr(mv[:, t, :], st[:, t, :]).then_inc(ln_aggr, 1)
    dve.wait_ge(ln_aggr, j * BT + BT)
    dve.tensor_scalar(ve[:], mv[:, :, 1], LN_EPS, None, ALU.add).then_inc(ln_var, 1)
    dve.wait_ge(rstd_done, j + 1)
    for t in range(BT):
        dve.tensor_scalar(z[:, t, :], x[:, bass.ds(j * BT + t, 1), :], mv[:, t, 0:1], rs[:, t:t + 1],
                          ALU.subtract, ALU.mult).then_inc(z_done, 1)


def ffn_phase(nc, tag, d, x, ident, first, split, out):
    with ExitStack() as ctx:
        def sb(name, shape, dt=F32):
            return ctx.enter_context(nc.sbuf_tensor(f"{tag}_{name}", shape, dt))

        def ps(name, shape):
            return ctx.enter_context(nc.psum_tensor(f"{tag}_{name}", shape, F32))

        def sem(name):
            return ctx.enter_context(nc.semaphore(f"{tag}_{name}"))

        e_raw = sb("e_raw", [P, E, C * D])
        e_hi, e_lo = sb("e_hi", [P, E, C * D], F32R), sb("e_lo", [P, E, C * D], F32R)
        p_raw = sb("p_raw", [P, C, D])
        p_hi, p_lo = sb("p_hi", [P, C, D], F32R), sb("p_lo", [P, C, D], F32R)
        r_raw = sb("r_raw", [P, C, E])
        r_hl = sb("r_hl", [P, C, P], F32R)
        r_h0 = sb("r_h0", [P, C, P], F32R)
        e_bias = sb("e_bias", [P, E * C])
        p_bias, n_w, r_bias = sb("p_bias", [P, D]), sb("n_w", [P, D]), sb("r_bias", [P, E])
        iota = sb("iota", [P, E])
        pick = sb("pick", [2 * E, E * P])
        pick_r = sb("pick_r", [2 * E, E, P], F32R)
        st, mv, ve, rs = sb("st", [P, BT, 6]), sb("mv", [P, BT, 2]), sb("ve", [P, BT]), sb("rs", [P, BT])
        mhalf = sb("mhalf", [P, BT])
        z = sb("z", [P, BT, D])
        zh, zl = sb("zh", [P, 2 * C, SEQ], F32R), sb("zl", [P, 2 * C, SEQ], F32R)
        zres = sb("zres", [P, 2 * BT, D])
        rT = sb("rT", [2 * E, SEQ])
        l0, lg = sb("l0", [P, BT, E]), sb("lg", [P, BT, E])
        top, topi = sb("top", [P, BT, 8]), sb("topi", [P, BT, 8], U32)
        topf = sb("topf", [P, BT, 2])
        gap, th = sb("gap", [P, BT]), sb("th", [P, BT])
        w0, w1 = sb("w0", [P, BT]), sb("w1", [P, BT])
        oh0, oh1 = sb("oh0", [P, BT, E]), sb("oh1", [P, BT, E])
        full = sb("full", [P, BT, E])
        full_hi = sb("full_hi", [P, BT, E], F32R)
        fw = sb("fw", [P, BT, P])
        wT = sb("wT", [2 * E, SEQ], F32R)
        s_ring = [sb(f"s{n}", [P, SEQ]) for n in range(4)]
        u_ring = [sb(f"u{n}", [P, SEQ]) for n in range(4)]
        acc = sb("acc", [P, C, SEQ])
        ch, cl = sb("ch", [P, C, SEQ], F32R), sb("cl", [P, C, SEQ], F32R)
        y, sq = sb("y", [P, BT, D]), sb("sq", [P, BT, D])
        ss, ms, rr = sb("ss", [P, BT]), sb("ms", [P, BT]), sb("rr", [P, BT])
        if first:
            kw = sb("kw", [P, HEADS])
            a_raw = sb("a_raw", [P, GW])
            a_hi, a_lo = sb("a_hi", [P, GW], F32R), sb("a_lo", [P, GW], F32R)

        ex_ps = [ps(f"ex{n}", [P, SEQ]) for n in range(4)]
        wb_ps = ps("wb", [P, SEQ])
        y_ps = ps("y_ps", [P, SEQ])
        t_ps = [ps(f"t{n}", [P, SEQ]) for n in range(2)]

        x_in = [sem(f"x_in{n}") for n in range(BATCH)]
        e_in = [sem(f"e_in{n}") for n in range(E)]
        small_in, pr_in = sem("small_in"), sem("pr_in")
        e_hi_done, e_lo_done, pr_split, setup, consts = (sem(n) for n in ("e_hi_done", "e_lo_done", "pr_split", "setup", "consts"))
        ln_stats, ln_aggr, ln_var, rstd_done, z_done = (sem(n) for n in ("ln_stats", "ln_aggr", "ln_var", "rstd_done", "z_done"))
        half_set = sem("half_set")
        passed = sem("passed")
        tz_done, zhi_done, zlo_done, zres_done = (sem(n) for n in ("tz_done", "zhi_done", "zlo_done", "zres_done"))
        rout_done, rT_done, tb_done, gate, tanh_done = (sem(n) for n in ("rout_done", "rT_done", "tb_done", "gate", "tanh_done"))
        gap_done, fw_done, tw_done, wT_done = (sem(n) for n in ("gap_done", "fw_done", "tw_done", "wT_done"))
        ex_done, silu_done, sel_done, mult_done, acc_done = (sem(n) for n in ("ex_done", "silu_done", "sel_done", "mult_done", "acc_done"))
        chi_done, clo_done, y_done, yadd_done, sq_done = (sem(n) for n in ("chi_done", "clo_done", "y_done", "yadd_done", "sq_done"))
        rms, rr_done, xn_done, x_done, out_done = (sem(n) for n in ("rms", "rr_done", "xn_done", "x_done", "out_done"))
        if first:
            a_in, a_scaled, a_hi_done, a_lo_done, a_out = (sem(n) for n in ("a_in", "a_scaled", "a_hi_done", "a_lo_done", "a_out"))

        RING = len(ex_ps)
        SILU0 = RING
        MULT0 = len(s_ring)
        YADD0 = 2
        X0 = 1
        GATE = 20
        EW = C * D

        block = ctx.enter_context(nc.Block())

        @block.sync
        def _(sp):
            if first:
                xr = d["x"].rearrange("(b t p) d -> b p t d", t=BT, p=P)
                for b in range(BATCH):
                    if b == 0:
                        sp.dma_start(x[:, 0:BT, :], xr[0]).then_inc(x_in[0], 16)
                        sp.dma_start(r_raw[:], d["router_w"]).then_inc(pr_in, 16)
                        sp.dma_start(p_raw[:], d["proj_w"]).then_inc(pr_in, 16)
                        for e in range(E):
                            sp.dma_start(e_raw[:, e, :], d["expert_w"][e]).then_inc(e_in[e], 16)
                    else:
                        sp.dma_start(x[:, b * BT:(b + 1) * BT, :], xr[b]).then_inc(x_in[b], 16)
            else:
                sp.dma_start(r_raw[:], d["router_w"]).then_inc(pr_in, 16)
                sp.dma_start(p_raw[:], d["proj_w"]).then_inc(pr_in, 16)
                for e in range(E):
                    sp.dma_start(e_raw[:, e, :], d["expert_w"][e]).then_inc(e_in[e], 16)

            def block_io(i):
                if first:
                    sp.dma_start(a_raw[:], d["attn_w"][bass.ds(i, 1)].rearrange("o p n -> (o p) n")).then_inc(a_in, 16)
                    sp.wait_ge(a_lo_done, i + 1).then_inc(passed, 1)
                    sp.dma_start(split[bass.ds(i, 1), 0].rearrange("o p n -> (o p) n"), a_hi[:].bitcast(F32)).then_inc(a_out, 16)
                    sp.dma_start(split[bass.ds(i, 1), 1].rearrange("o p n -> (o p) n"), a_lo[:].bitcast(F32)).then_inc(a_out, 16)
                    sp.wait_ge(a_out, 32 * i + 32).then_inc(passed, 1)
                if out is not None:
                    sp.wait_ge(x_done, X0 + i + 1).then_inc(passed, 1)
                    sp.dma_start(out.rearrange("(b t p) d -> b p t d", t=BT, p=P)[bass.ds(i, 1)].rearrange("o p t d -> (o p) t d"),
                                 x[:, bass.ds(i * BT, BT), :]).then_inc(out_done, 16)

            with sp.Fori(0, BATCH) as i:
                block_io(i)
            if out is not None:
                sp.wait_ge(out_done, 16 * BATCH)

        @block.gpsimd
        def _(pool):
            pool.sem_inc(x_done, X0)
            pool.memset(mhalf[:], -0.5).then_inc(half_set, 1)
            pool.dma_start(p_bias[:], d["proj_b"].partition_broadcast(P)).then_inc(small_in, 16)
            pool.dma_start(n_w[:], d["norm_w"].partition_broadcast(P)).then_inc(small_in, 16)
            pool.dma_start(r_bias[:], d["router_b"].partition_broadcast(P)).then_inc(small_in, 16)
            pool.dma_start(iota[:], d["iota"].partition_broadcast(P)).then_inc(small_in, 16)
            pool.dma_start(e_bias[:], d["expert_b"]).then_inc(small_in, 16)
            pool.dma_start(pick[:], d["pick"]).then_inc(small_in, 16)
            if first:
                pool.dma_start(ident[:], d["ident"]).then_inc(small_in, 16)
                pool.dma_start(kw[:], d["key_weights"].partition_broadcast(P)).then_inc(small_in, 16)
            pool.wait_ge(small_in, 16 * (8 if first else 6))

            def rstd(j):
                pool.wait_ge(ln_var, j + 1)
                pool.tensor_tensor(rs[:], ve[:], mhalf[:], ALU.pow).then_inc(rstd_done, 1)

            def residual(j):
                pool.wait_ge(z_done, BT * j + BT)
                pool.tensor_tensor(zres[:, bass.ds((j % 2) * BT, BT), :], z[:],
                                   p_bias[:].unsqueeze(1).to_broadcast([P, BT, D]), ALU.add).then_inc(zres_done, 1)

            def body(i, more):
                if more:
                    rstd(i + 1)
                if first:
                    pool.wait_ge(consts, 2)
                    pool.wait_ge(a_in, 16 * i + 16)
                    for c in range(C):
                        q = a_raw[:, c * QKV:c * QKV + G * HD].rearrange("p (h d) -> p h d", h=G)
                        pool.tensor_tensor(q, q, kw[:, bass.ds(i * G, G)].unsqueeze(2).to_broadcast([P, G, HD]),
                                           ALU.mult).then_inc(a_scaled, 1)
                for e in range(1, E):
                    for f in range(C):
                        n = C * e + f
                        pool.wait_ge(mult_done, MULT0 + 2 * E * i + n + 1)
                        if e > 1:
                            pool.wait_ge(acc_done, 2 * (E - 1) * i + 2 * (e - 2) + f + 1)
                        pool.tensor_tensor(acc[:, f, :], acc[:, f, :], u_ring[n % 4][:], ALU.add).then_inc(acc_done, 1)
                    if e == 1 and more:
                        residual(i + 1)
                pool.wait_ge(rms, i + 1)
                pool.tensor_tensor(rr[:], ms[:], mhalf[:], ALU.pow).then_inc(rr_done, 1)
                pool.wait_ge(xn_done, BT * i + BT)
                xb = x[:, bass.ds(i * BT, BT), :]
                pool.tensor_tensor(xb, xb, y[:], ALU.add).then_inc(x_done, 1)

            pool.wait_ge(half_set, 1)
            rstd(0)
            residual(0)
            with pool.Fori(0, BATCH - 1) as i:
                body(i, True)
            body(BATCH - 1, False)

        @block.vector
        def _(dve):
            dve.sem_inc(mult_done, MULT0)
            dve.sem_inc(yadd_done, YADD0)
            dve.memset(fw[:], 0.0).then_inc(setup, 1)
            dve.memset(r_hl[:].bitcast(F32), 0.0).then_inc(setup, 1)
            dve.memset(r_h0[:].bitcast(F32), 0.0).then_inc(setup, 1)

            def norm(j):
                layer_norm_block(dve, x, j, st, mv, ve, rs, z, ln_stats, ln_aggr, ln_var, rstd_done, z_done, passed)

            def z_rest(j):
                for c in range(C):
                    dve.wait_ge(zhi_done, C * j + c + 1)
                    k = bass.ds((j % 2) * C + c, 1)
                    dve.tensor_tensor(zl[:, k, :], t_ps[c][:].unsqueeze(1), zh[:, k, :].bitcast(F32),
                                      ALU.subtract).then_inc(zlo_done, 1)

            def gating(j):
                g = GATE * j
                lp = t_ps[1][:, 0:BT * 2 * E].rearrange("p (t k) -> p t k", t=BT)
                dve.wait_ge(tb_done, j + 1)
                dve.tensor_tensor(l0[:], lp[:, :, E:2 * E], r_bias[:].unsqueeze(1).to_broadcast([P, BT, E]),
                                  ALU.add).then_inc(gate, 1)
                dve.wait_ge(gate, g + 1)
                dve.tensor_tensor(lg[:], lp[:, :, 0:E], l0[:], ALU.add).then_inc(gate, 1)
                dve.wait_ge(gate, g + 2).then_inc(passed, 1)
                for t in range(BT):
                    dve.max(top[:, t, :], lg[:, t, :]).then_inc(gate, 1)
                dve.wait_ge(gate, g + 6)
                dve.tensor_tensor(gap[:].unsqueeze(2), top[:, :, 0:1], top[:, :, 1:2], ALU.subtract).then_inc(gap_done, 1)
                for t in range(BT):
                    dve.max_index(topi[:, t, :], top[:, t, :], lg[:, t, :]).then_inc(gate, 1)
                dve.wait_ge(gate, g + 10)
                dve.tensor_copy(topf[:], topi[:, :, 0:2]).then_inc(gate, 1)
                dve.wait_ge(gate, g + 11)
                io = iota[:].unsqueeze(1).to_broadcast([P, BT, E])
                dve.tensor_tensor(oh0[:], io, topf[:, :, 0:1].to_broadcast([P, BT, E]), ALU.is_equal).then_inc(gate, 1)
                dve.tensor_tensor(oh1[:], io, topf[:, :, 1:2].to_broadcast([P, BT, E]), ALU.is_equal).then_inc(gate, 1)
                dve.wait_ge(tanh_done, j + 1)
                dve.tensor_scalar(w0[:], th[:], 0.5, 0.5, ALU.mult, ALU.add).then_inc(gate, 1)
                dve.tensor_scalar(w1[:], th[:], -0.5, 0.5, ALU.mult, ALU.add).then_inc(gate, 1)
                dve.wait_ge(gate, g + 15)
                dve.tensor_tensor(oh0[:], oh0[:], w0[:].unsqueeze(2).to_broadcast([P, BT, E]), ALU.mult).then_inc(gate, 1)
                dve.tensor_tensor(oh1[:], oh1[:], w1[:].unsqueeze(2).to_broadcast([P, BT, E]), ALU.mult).then_inc(gate, 1)
                dve.wait_ge(gate, g + 17)
                dve.tensor_tensor(full[:], oh0[:], oh1[:], ALU.add).then_inc(gate, 1)
                dve.wait_ge(gate, g + 18)
                dve.tensor_copy(full_hi[:], full[:]).then_inc(gate, 1)
                dve.wait_ge(gate, g + 19)
                dve.tensor_copy(fw[:, :, 0:E], full_hi[:].bitcast(F32)).then_inc(gate, 1)
                dve.tensor_tensor(fw[:, :, E:2 * E], full[:], full_hi[:].bitcast(F32), ALU.subtract).then_inc(fw_done, 1)

            def body(i, more):
                if more:
                    dve.wait_ge(zres_done, i + 1)
                    norm(i + 1)
                for e in range(E):
                    for f in range(C):
                        n = C * e + f
                        dve.wait_ge(silu_done, SILU0 + 2 * E * i + n + 1)
                        if f == 0:
                            dve.wait_ge(sel_done, E * i + e + 1)
                        if e >= 3:
                            dve.wait_ge(acc_done, 2 * (E - 1) * i + 2 * (e - 3) + f + 1)
                        to = acc[:, f, :] if e == 0 else u_ring[n % 4][:]
                        dve.tensor_tensor(to, s_ring[n % 4][:], wb_ps[:], ALU.mult).then_inc(mult_done, 1)
                    if first and e == 1:
                        for half in range(2):
                            cols = slice(half * GW // 2, (half + 1) * GW // 2)
                            dve.wait_ge(a_hi_done, 2 * i + half + 1)
                            r = dve.tensor_tensor(a_lo[:, cols], a_raw[:, cols], a_hi[:, cols].bitcast(F32), ALU.subtract)
                        r.then_inc(a_lo_done, 1)
                    if more and e == 3:
                        z_rest(i + 1)
                    if more and e == 6:
                        gating(i + 1)
                for f in range(C):
                    dve.wait_ge(chi_done, C * i + f + 1)
                    dve.tensor_tensor(cl[:, f, :], acc[:, f, :], ch[:, f, :].bitcast(F32), ALU.subtract).then_inc(clo_done, 1)
                dve.wait_ge(x_done, X0 + i)
                dve.wait_ge(zres_done, i + 1)
                for u in range(2):
                    dve.wait_ge(y_done, 2 * i + u + 1)
                    src = (y_ps, wb_ps)[u][:].rearrange("p (t d) -> p t d", t=2)
                    dve.tensor_tensor(y[:, 2 * u:2 * u + 2, :], src, zres[:, bass.ds((i % 2) * BT + 2 * u, 2), :],
                                      ALU.add).then_inc(yadd_done, 1)
                dve.wait_ge(sq_done, BT * i + BT)
                dve.tensor_scalar(ms[:], ss[:], 1.0 / D, RMS_EPS, ALU.mult, ALU.add).then_inc(rms, 1)
                dve.wait_ge(rr_done, i + 1)
                for t in range(BT):
                    dve.scalar_tensor_tensor(out=y[:, t, :], in0=y[:, t, :], scalar=rr[:, t:t + 1], in1=n_w[:],
                                             op0=ALU.mult, op1=ALU.mult).then_inc(xn_done, 1)

            if first:
                dve.wait_ge(x_in[0], 16)
            norm(0)
            dve.wait_ge(small_in, 16 * (8 if first else 6))
            dve.wait_ge(setup, 3)
            dve.tensor_scalar(n_w[:], n_w[:], 0.5, None, ALU.mult).then_inc(consts, 1)
            if first:
                dve.tensor_scalar(kw[:], kw[:], -float(HD) ** -0.5, None, ALU.mult).then_inc(consts, 1)
            dve.tensor_copy(pick_r[:].rearrange("k e p -> k (e p)"), pick[:]).then_inc(setup, 1)
            dve.wait_ge(pr_in, 32)
            dve.tensor_copy(r_hl[:, :, 0:E], r_raw[:]).then_inc(pr_split, 1)
            dve.tensor_copy(r_h0[:, :, 0:E], r_raw[:]).then_inc(pr_split, 1)
            dve.wait_ge(pr_split, 2)
            dve.tensor_tensor(r_hl[:, :, E:2 * E], r_raw[:], r_hl[:, :, 0:E].bitcast(F32), ALU.subtract).then_inc(pr_split, 1)
            z_rest(0)
            for e in range(E):
                dve.wait_ge(e_hi_done, e + 1)
                dve.tensor_tensor(e_lo[:, e, :], e_raw[:, e, :], e_hi[:, e, :].bitcast(F32), ALU.subtract).then_inc(e_lo_done, 1)
                if e == 3:
                    gating(0)
            dve.wait_ge(e_hi_done, E + 1)
            dve.tensor_tensor(p_lo[:], p_raw[:], p_hi[:].bitcast(F32), ALU.subtract).then_inc(pr_split, 1)
            if first:
                for b in range(1, BATCH):
                    dve.wait_ge(x_in[b], 16)
            with dve.Fori(0, BATCH - 1) as i:
                body(i, True)
            body(BATCH - 1, False)

        @block.scalar
        def _(act):
            act.sem_inc(silu_done, SILU0)

            def z_lead(j):
                for c in range(C):
                    act.wait_ge(tz_done, C * j + c + 1)
                    act.activation(zh[:, bass.ds((j % 2) * C + c, 1), :], t_ps[c][:].unsqueeze(1),
                                   ACT.Copy).then_inc(zhi_done, 1)

            def logits_out(j):
                act.wait_ge(rout_done, j + 1)
                act.activation(rT[:], t_ps[0][0:2 * E, :], ACT.Copy).then_inc(rT_done, 1)

            def half_tanh(j):
                act.wait_ge(gap_done, j + 1)
                act.activation(th[:], gap[:], ACT.Tanh, scale=0.5).then_inc(tanh_done, 1)

            def weights_out(j):
                act.wait_ge(tw_done, j + 1)
                act.activation(wT[:], t_ps[0][0:2 * E, :], ACT.Copy).then_inc(wT_done, 1)

            def body(i, more):
                for e in range(E):
                    for f in range(C):
                        n = C * e + f
                        act.wait_ge(ex_done, 2 * E * i + n + 1)
                        act.wait_ge(mult_done, 2 * E * i + n + 1)
                        act.activation(s_ring[n % 4][:], ex_ps[n % RING][:], ACT.Silu,
                                       bias=e_bias[:, n:n + 1]).then_inc(silu_done, 1)
                    if first and e == 0:
                        act.wait_ge(a_scaled, 2 * i + 2)
                        for half in range(2):
                            cols = slice(half * GW // 2, (half + 1) * GW // 2)
                            act.activation(a_hi[:, cols], a_raw[:, cols], ACT.Copy).then_inc(a_hi_done, 1)
                    if more and e == 2:
                        z_lead(i + 1)
                    if more and e == 4:
                        logits_out(i + 1)
                    if more and e == 6:
                        half_tanh(i + 1)
                for f in range(C):
                    act.wait_ge(acc_done, 2 * (E - 1) * i + 2 * (E - 2) + f + 1)
                    act.activation(ch[:, f, :], acc[:, f, :], ACT.Copy).then_inc(chi_done, 1)
                if more:
                    weights_out(i + 1)
                for t in range(BT):
                    act.wait_ge(yadd_done, YADD0 + 2 * i + t // 2 + 1)
                    act.activation(sq[:, t, :], y[:, t, :], ACT.Square, accum_out=ss[:, t:t + 1]).then_inc(sq_done, 1)

            z_lead(0)
            for e in range(2):
                act.wait_ge(e_in[e], 16)
                act.activation(e_hi[:, e, :], e_raw[:, e, :], ACT.Copy).then_inc(e_hi_done, 1)
            logits_out(0)
            for e in range(2, 4):
                act.wait_ge(e_in[e], 16)
                act.activation(e_hi[:, e, :], e_raw[:, e, :], ACT.Copy).then_inc(e_hi_done, 1)
            half_tanh(0)
            for e in range(4, E):
                act.wait_ge(e_in[e], 16)
                act.activation(e_hi[:, e, :], e_raw[:, e, :], ACT.Copy).then_inc(e_hi_done, 1)
            act.wait_ge(pr_in, 32)
            act.activation(p_hi[:], p_raw[:], ACT.Copy).then_inc(e_hi_done, 1)
            weights_out(0)
            act.wait_ge(small_in, 16 * (8 if first else 6))
            with act.Fori(0, BATCH - 1) as i:
                body(i, True)
            body(BATCH - 1, False)

        @block.tensor
        def _(pe):
            def transpose_z(j):
                pe.wait_ge(z_done, BT * j + BT)
                for c in range(C):
                    for t in range(BT):
                        r = pe.transpose(t_ps[c][:, t * P:(t + 1) * P], z[:, t, c * P:(c + 1) * P], ident[:])
                    r.then_inc(tz_done, 1)

            def router(j):
                pe.wait_ge(zlo_done, C * j + C)
                for c in range(C):
                    k = bass.ds((j % 2) * C + c, 1)
                    pe.matmul(t_ps[0][:], r_hl[:, c, :], zh[:, k, :].rearrange("p o s -> p (o s)"), start=(c == 0), stop=False)
                    r = pe.matmul(t_ps[0][:], r_h0[:, c, :], zl[:, k, :].rearrange("p o s -> p (o s)"), start=False, stop=(c == C - 1))
                r.then_inc(rout_done, 1)

            def logits_back(j):
                pe.wait_ge(rT_done, j + 1).then_inc(passed, 1)
                for t in range(BT):
                    r = pe.transpose(t_ps[1][:, t * 2 * E:(t + 1) * 2 * E], rT[:, t * P:(t + 1) * P], ident[0:2 * E, 0:2 * E])
                r.then_inc(tb_done, 1)

            def weights_T(j):
                pe.wait_ge(fw_done, j + 1)
                for t in range(BT):
                    r = pe.transpose(t_ps[0][:, t * P:(t + 1) * P], fw[:, t, :], ident[:])
                r.then_inc(tw_done, 1)

            def body(i, more):
                for e in range(E):
                    for f in range(C):
                        n = C * e + f
                        pe.wait_ge(silu_done, 2 * E * i + n + 1)
                        bank = ex_ps[n % RING][:]
                        for c in range(C):
                            k = bass.ds((i % 2) * C + c, 1)
                            w = slice(c * D + f * P, c * D + (f + 1) * P)
                            h, l = (v[:, k, :].rearrange("p o s -> p (o s)") for v in (zh, zl))
                            pe.matmul(bank, e_hi[:, e, w], h, start=(c == 0), stop=False)
                            pe.matmul(bank, e_hi[:, e, w], l, start=False, stop=False)
                            r = pe.matmul(bank, e_lo[:, e, w], h, start=False, stop=(c == C - 1))
                        r.then_inc(ex_done, 1)
                    if e == 0:
                        pe.wait_ge(wT_done, i + 1)
                        pe.wait_ge(yadd_done, 2 * i + 2)
                    else:
                        pe.wait_ge(mult_done, MULT0 + 2 * E * i + C * e)
                    pe.matmul(wb_ps[:], pick_r[:, e, :], wT[:], start=True, stop=True).then_inc(sel_done, 1)
                    if more and e == 1:
                        transpose_z(i + 1)
                    if more and e == 3:
                        router(i + 1)
                    if more and e == 4:
                        logits_back(i + 1)
                if more:
                    weights_T(i + 1)
                pe.wait_ge(clo_done, C * i + C)
                for u in range(2):
                    bank = (y_ps, wb_ps)[u]
                    for t in range(2):
                        tok = slice((2 * u + t) * P, (2 * u + t + 1) * P)
                        o = bank[:, t * D:(t + 1) * D]
                        for f in range(C):
                            pe.matmul(o, ch[:, f, tok], p_hi[:, f, :], start=(f == 0), stop=False)
                            pe.matmul(o, ch[:, f, tok], p_lo[:, f, :], start=False, stop=False)
                            r = pe.matmul(o, cl[:, f, tok], p_hi[:, f, :], start=False, stop=(f == C - 1))
                    r.then_inc(y_done, 1)

            pe.wait_ge(small_in, 16 * (8 if first else 6))
            transpose_z(0)
            pe.wait_ge(setup, 4)
            pe.wait_ge(pr_split, 3)
            router(0)
            logits_back(0)
            weights_T(0)
            for e in range(E):
                pe.wait_ge(e_lo_done, e + 1)
            pe.wait_ge(pr_split, 4)
            with pe.Fori(0, BATCH - 1) as i:
                body(i, True)
            body(BATCH - 1, False)


def attention_phase(nc, d, x, ident, split):
    with ExitStack() as ctx:
        def sb(name, shape, dt=F32):
            return ctx.enter_context(nc.sbuf_tensor(f"at_{name}", shape, dt))

        def ps(name, shape):
            return ctx.enter_context(nc.psum_tensor(f"at_{name}", shape, F32))

        def sem(name):
            return ctx.enter_context(nc.semaphore(f"at_{name}"))

        STEPS = KV * BATCH
        NR = G + 1
        OFF = [P * (i * (i + 1) // 2) for i in range(BT)]
        TRI = OFF[-1] + BT * P
        QT = (3, 2, 0, 1)
        FILL = (((0, 0, 4 * P),), ((1, 0, 3 * P), (3, 3 * P, P)), ((2, 0, 2 * P),))
        FCOL, FLEN = (0, SEQ, 2 * SEQ), (SEQ, SEQ, 2 * P)

        zh, zl = sb("zh", [P, C, TOKENS], F32R), sb("zl", [P, C, TOKENS], F32R)
        cosT, sinT, mask = sb("cos", [P, SEQ]), sb("sin", [P, SEQ]), sb("mask", [P, SEQ])
        st, mv, ve, rs = sb("st", [P, BT, 6]), sb("mv", [P, BT, 2]), sb("ve", [P, BT]), sb("rs", [P, BT])
        mhalf = sb("mhalf", [P, BT])
        z = sb("z", [P, BT, D])
        wqkv = [sb(f"wqkv{n}", [P, C, QKV], F32R) for n in range(2)]
        wo = [sb(f"wo{n}", [P, G, D], F32R) for n in range(2)]
        raw = [sb(f"raw{n}", [P, SEQ]) for n in range(2)]
        swap = [sb(f"swap{n}", [P, SEQ]) for n in range(2)]
        rot = [sb(f"rot{n}", [P, SEQ]) for n in range(2)]
        rot2 = [sb(f"rot2{n}", [P, SEQ]) for n in range(2)]
        qh, ql = sb("qh", [P, NR, SEQ], F32R), sb("ql", [P, NR, SEQ], F32R)
        vT = sb("vT", [P, SEQ])
        vh, vl = sb("vh", [P, BT, HD], F32R), sb("vl", [P, BT, HD], F32R)
        sm = [sb(f"sm{n}", [P, TRI]) for n in range(2)]
        pr = [sb(f"pr{n}", [P, TRI]) for n in range(2)]
        low, tot, inv = ([sb(f"{n}{k}", [P, BT]) for k in range(2)] for n in ("low", "tot", "inv"))
        pth, ptl = sb("pth", [P, TRI], F32R), sb("ptl", [P, TRI], F32R)
        oh, ol = sb("oh", [P, G, SEQ], F32R), sb("ol", [P, G, SEQ], F32R)

        pj = [ps(f"pj{n}", [P, SEQ]) for n in range(2)]
        sc = [ps(f"sc{n}", [P, SEQ]) for n in range(3)]
        pt = [ps(f"pt{n}", [P, SEQ]) for n in range(2)]
        o_ps = ps("o", [P, SEQ])
        PLACE = {3: (0, 0), 2: (1, 0), 0: (1, 3 * P), 1: (2, 0)}

        const_in, wqkv_in, wo_in = sem("const_in"), sem("wqkv_in"), sem("wo_in")
        swap_in = [sem(f"swap_in{n}") for n in range(2)]
        ln_stats, ln_aggr, ln_var, rstd_done, z_done = (sem(n) for n in ("ln_stats", "ln_aggr", "ln_var", "rstd_done", "z_done"))
        half_set = sem("half_set")
        passed = sem("passed")
        tz_done, zhi_done, zlo_done = (sem(n) for n in ("tz_done", "zhi_done", "zlo_done"))
        pj_ready, sc_ready, pt_ready, o_ready = (sem(n) for n in ("pj_ready", "sc_ready", "pt_ready", "o_ready"))
        raw_done, qh_done, vt_done, vh_done, vl_done = (sem(n) for n in ("raw_done", "qh_done", "vt_done", "vh_done", "vl_done"))
        ex_done, hi_done, lo_done, oh_done, ol_done = (sem(n) for n in ("ex_done", "hi_done", "lo_done", "oh_done", "ol_done"))
        mx_done, inv_done, nm_done, xu_done = (sem(n) for n in ("mx_done", "inv_done", "nm_done", "xu_done"))
        cos_done, sin_done, sum_done, ql_done = (sem(n) for n in ("cos_done", "sin_done", "sum_done", "ql_done"))

        LO0 = 2
        OL0 = 1
        K, Q0, Q1, V, Q2, VT, Q3, WO0, WO1 = range(9)
        FILLS = 9
        QFILL = (K, Q0, Q1, Q2, Q3)

        def proj_fill(s, k):
            return k + 1 if isinstance(s, int) and s == 0 else FILLS * (s - 1) + 7 + k + 1

        def wo_fill(s, u, last):
            return FILLS * s + 7 + (0 if last else 7) + u + 1

        block = ctx.enter_context(nc.Block())

        @block.sync
        def _(sp):
            sp.dma_start(cosT[:], d["rope_cos"]).then_inc(const_in, 16)
            sp.dma_start(sinT[:], d["rope_sin"]).then_inc(const_in, 16)
            sp.dma_start(mask[:], d["mask"]).then_inc(const_in, 16)

            def load_qkv(g):
                for n in range(2):
                    sp.dma_start(wqkv[n][:].rearrange("p c n -> p (c n)").bitcast(F32),
                                 split[bass.ds(g, 1), n, :, 0:C * QKV].rearrange("o p n -> (o p) n")).then_inc(wqkv_in, 16)

            def load_wo(g):
                for n in range(2):
                    sp.dma_start(wo[n][:].rearrange("p h n -> p (h n)").bitcast(F32),
                                 split[bass.ds(g, 1), n, :, C * QKV:GW].rearrange("o p n -> (o p) n")).then_inc(wo_in, 16)

            def swaps(s):
                for r in range(NR):
                    b = r % 2
                    sp.wait_ge(raw_done, NR * s + r + 1)
                    sp.dma_start(swap[b][0:HD // 2, :], raw[b][HD // 2:HD, :]).then_inc(swap_in[b], 16)
                    sp.dma_start(swap[b][HD // 2:HD, :], raw[b][0:HD // 2, :]).then_inc(swap_in[b], 16)

            load_qkv(0)
            load_wo(0)
            with sp.Fori(0, BATCH) as b:
                swaps(b)
            with sp.Fori(1, KV) as g:
                s = g * BATCH
                sp.wait_ge(pj_ready, proj_fill(s - 1, Q3)).then_inc(passed, 1)
                load_qkv(g)
                swaps(s)
                sp.wait_ge(pj_ready, wo_fill(s - 1, 1, False)).then_inc(passed, 1)
                load_wo(g)
                with sp.Fori(1, BATCH) as b:
                    swaps(s + b)

        @block.gpsimd
        def _(pool):
            def rest(s, r):
                b = r % 2
                pool.wait_ge(qh_done, NR * s + r + 1)
                pool.tensor_tensor(ql[:, r, :], rot[b][:], qh[:, r, :].bitcast(F32), ALU.subtract).then_inc(ql_done, 1)

            def rope(s):
                for r in range(NR):
                    b = r % 2
                    pool.wait_ge(raw_done, NR * s + r + 1)
                    if r >= 2:
                        pool.wait_ge(ql_done, NR * s + r - 1)
                    elif not isinstance(s, int):
                        pool.wait_ge(ql_done, NR * s)
                    pool.tensor_tensor(rot[b][:], raw[b][:], cosT[:], ALU.mult).then_inc(cos_done, 1)
                    if r > 0:
                        rest(s, r - 1)
                    pool.wait_ge(swap_in[b], 32 * ((NR + 1 - b) // 2 * s + r // 2 + 1))
                    pool.tensor_tensor(rot2[b][:], swap[b][:], sinT[:], ALU.mult).then_inc(sin_done, 1)
                    pool.wait_ge(sin_done, NR * s + r + 1)
                    pool.tensor_tensor(rot[b][:], rot[b][:], rot2[b][:], ALU.add).then_inc(sum_done, 1)
                rest(s, NR - 1)

            def rstd(j):
                pool.wait_ge(ln_var, j + 1)
                pool.tensor_tensor(rs[:], ve[:], mhalf[:], ALU.pow).then_inc(rstd_done, 1)

            pool.memset(mhalf[:], -0.5).then_inc(half_set, 1)
            pool.wait_ge(half_set, 1)
            rstd(0)
            with pool.Fori(1, BATCH) as j:
                rstd(j)
            pool.wait_ge(const_in, 48)
            rope(0)
            with pool.Fori(1, STEPS) as s:
                rope(s)

        @block.vector
        def _(dve):
            dve.sem_inc(lo_done, LO0)
            dve.sem_inc(ol_done, OL0)

            def z_rest(j):
                for c in range(C):
                    dve.wait_ge(zhi_done, C * j + c + 1)
                    cols = bass.ds(j * SEQ, SEQ)
                    dve.tensor_tensor(zl[:, c, cols], pj[c][:], zh[:, c, cols].bitcast(F32), ALU.subtract).then_inc(zlo_done, 1)

            def mask_min(n, h, tiles=QT):
                for i in tiles:
                    k = QT.index(i)
                    bank, col = PLACE[i]
                    if k == 0 and not (isinstance(n, int) and n < 2):
                        dve.wait_ge(ex_done, BT * (n - 1)).then_inc(passed, 1)
                    dve.wait_ge(sc_ready, 3 * n + bank + 1).then_inc(passed, 1)
                    w = (i + 1) * P
                    dve.tensor_tensor_reduce(out=sm[h % 2][:, OFF[i]:OFF[i] + w], in0=sc[bank][:, col:col + w],
                                             in1=mask[:, SEQ - w:SEQ], scale=1.0, scalar=3e38, op0=ALU.add, op1=ALU.min,
                                             accum_out=low[h % 2][:, i:i + 1]).then_inc(mx_done, 1)

            def normalise(n, h):
                dve.wait_ge(ex_done, BT * n + BT)
                dve.reciprocal(inv[h % 2][:], tot[h % 2][:]).then_inc(inv_done, 1)
                dve.wait_ge(inv_done, n + 1)
                for i in range(BT):
                    a = pr[h % 2][:, OFF[i]:OFF[i] + (i + 1) * P]
                    dve.tensor_scalar(a, a, inv[h % 2][:, i:i + 1], None, ALU.mult).then_inc(nm_done, 1)

            def prob_rest(s, h, k):
                q = 3 * G * s + 3 * h + k
                dve.wait_ge(hi_done, q + 1)
                cols = slice(FCOL[k], FCOL[k] + FLEN[k])
                dve.tensor_tensor(ptl[:, cols], pt[(3 * h + k) % 2][:, 0:FLEN[k]], pth[:, cols].bitcast(F32),
                                  ALU.subtract).then_inc(lo_done, 1)

            def out_rest(s, h):
                dve.wait_ge(oh_done, G * s + h + 1)
                dve.tensor_tensor(ol[:, h, :], o_ps[:], oh[:, h, :].bitcast(F32), ALU.subtract).then_inc(ol_done, 1)

            def value_rest(s):
                dve.wait_ge(vh_done, s + 1)
                dve.tensor_tensor(vl[:].rearrange("p t d -> p (t d)"), pj[1][:], vh[:].rearrange("p t d -> p (t d)").bitcast(F32),
                                  ALU.subtract).then_inc(vl_done, 1)

            def step(s, last):
                n = G * s
                prob_rest(s, 0, 0)
                prob_rest(s, 0, 1)
                mask_min(n + 2, 2)
                prob_rest(s, 0, 2)
                out_rest(s, 0)
                prob_rest(s, 1, 0)
                prob_rest(s, 1, 1)
                normalise(n + 2, 2)
                mask_min(n + 3, 3)
                prob_rest(s, 1, 2)
                out_rest(s, 1)
                prob_rest(s, 2, 0)
                prob_rest(s, 2, 1)
                normalise(n + 3, 3)
                prob_rest(s, 2, 2)
                out_rest(s, 2)
                prob_rest(s, 3, 0)
                prob_rest(s, 3, 1)
                if not last:
                    mask_min(n + 4, 0)
                prob_rest(s, 3, 2)
                out_rest(s, 3)
                if not last:
                    value_rest(s + 1)
                    normalise(n + 4, 0)
                    mask_min(n + 5, 1)
                    normalise(n + 5, 1)
                for u in range(2):
                    dve.wait_ge(pj_ready, wo_fill(s, u, last))
                    xb = x[:, bass.ds((s % BATCH) * BT + 2 * u, 2), :]
                    dve.tensor_tensor(xb, pj[1 - u][:].rearrange("p (t d) -> p t d", t=2), xb, ALU.add).then_inc(xu_done, 1)

            layer_norm_block(dve, x, 0, st, mv, ve, rs, z, ln_stats, ln_aggr, ln_var, rstd_done, z_done, passed)
            z_rest(0)
            with dve.Fori(1, BATCH) as j:
                layer_norm_block(dve, x, j, st, mv, ve, rs, z, ln_stats, ln_aggr, ln_var, rstd_done, z_done, passed)
                z_rest(j)
            dve.wait_ge(const_in, 48)
            mask_min(0, 0)
            value_rest(0)
            normalise(0, 0)
            mask_min(1, 1)
            normalise(1, 1)
            with dve.Fori(0, STEPS - 1) as s:
                step(s, False)
            step(STEPS - 1, True)

        @block.scalar
        def _(act):
            def z_lead(j):
                for c in range(C):
                    act.wait_ge(tz_done, C * j + c + 1)
                    act.activation(zh[:, c, bass.ds(j * SEQ, SEQ)], pj[c][:], ACT.Copy).then_inc(zhi_done, 1)

            def raw_out(s, r):
                act.wait_ge(pj_ready, proj_fill(s, QFILL[r]))
                if r >= 2:
                    act.wait_ge(sin_done, NR * s + r - 1)
                elif not isinstance(s, int):
                    act.wait_ge(sin_done, NR * s)
                act.activation(raw[r % 2][:], pj[QFILL[r] % 2 if QFILL[r] < Q2 else 0][:], ACT.Copy).then_inc(raw_done, 1)

            def rotated_lead(s, r):
                act.wait_ge(sum_done, NR * s + r + 1)
                act.activation(qh[:, r, :], rot[r % 2][:], ACT.Copy).then_inc(qh_done, 1)

            def value_out(s):
                act.wait_ge(pj_ready, proj_fill(s, V))
                act.activation(vT[:], pj[1][:], ACT.Copy).then_inc(vt_done, 1)

            def value_lead(s):
                act.wait_ge(pj_ready, proj_fill(s, VT))
                act.activation(vh[:].rearrange("p t d -> p (t d)"), pj[1][:], ACT.Copy).then_inc(vh_done, 1)

            def exps(n, h, tiles=QT):
                for i in tiles:
                    k = QT.index(i)
                    act.wait_ge(mx_done, BT * n + k + 1)
                    if k == 0 and not (isinstance(n, int) and n < 2):
                        act.wait_ge(pt_ready, 3 * (n - 1))
                    cols = slice(OFF[i], OFF[i] + (i + 1) * P)
                    act.activation(pr[h % 2][:, cols], sm[h % 2][:, cols], ACT.Exp, bias=low[h % 2][:, i:i + 1],
                                   scale=-1.0, accum_out=tot[h % 2][:, i:i + 1]).then_inc(ex_done, 1)

            def prob_lead(s, h, k):
                act.wait_ge(pt_ready, 3 * G * s + 3 * h + k + 1)
                cols = slice(FCOL[k], FCOL[k] + FLEN[k])
                act.activation(pth[:, cols], pt[(3 * h + k) % 2][:, 0:FLEN[k]], ACT.Copy).then_inc(hi_done, 1)

            def out_lead(s, h):
                act.wait_ge(o_ready, G * s + h + 1)
                act.activation(oh[:, h, :], o_ps[:], ACT.Copy).then_inc(oh_done, 1)

            def step(s, last):
                n = G * s
                prob_lead(s, 0, 0)
                prob_lead(s, 0, 1)
                exps(n + 2, 2, QT[:1])
                prob_lead(s, 0, 2)
                exps(n + 2, 2, QT[1:])
                out_lead(s, 0)
                prob_lead(s, 1, 0)
                prob_lead(s, 1, 1)
                exps(n + 3, 3, QT[:1])
                prob_lead(s, 1, 2)
                exps(n + 3, 3, QT[1:])
                out_lead(s, 1)
                if not last:
                    raw_out(s + 1, 0)
                prob_lead(s, 2, 0)
                prob_lead(s, 2, 1)
                if not last:
                    raw_out(s + 1, 1)
                prob_lead(s, 2, 2)
                if not last:
                    rotated_lead(s + 1, 0)
                out_lead(s, 2)
                if not last:
                    raw_out(s + 1, 2)
                    value_out(s + 1)
                    rotated_lead(s + 1, 1)
                prob_lead(s, 3, 0)
                prob_lead(s, 3, 1)
                if not last:
                    exps(n + 4, 0, QT[:1])
                prob_lead(s, 3, 2)
                if not last:
                    exps(n + 4, 0, QT[1:])
                    rotated_lead(s + 1, 2)
                out_lead(s, 3)
                if not last:
                    raw_out(s + 1, 3)
                    value_lead(s + 1)
                    exps(n + 5, 1)
                    raw_out(s + 1, 4)
                    rotated_lead(s + 1, 3)
                    rotated_lead(s + 1, 4)

            z_lead(0)
            with act.Fori(1, BATCH) as j:
                z_lead(j)
            raw_out(0, 0)
            raw_out(0, 1)
            rotated_lead(0, 0)
            raw_out(0, 2)
            value_out(0)
            rotated_lead(0, 1)
            exps(0, 0)
            rotated_lead(0, 2)
            raw_out(0, 3)
            value_lead(0)
            exps(1, 1)
            raw_out(0, 4)
            rotated_lead(0, 3)
            rotated_lead(0, 4)
            with act.Fori(0, STEPS - 1) as s:
                step(s, False)
            step(STEPS - 1, True)

        @block.tensor
        def _(pe):
            def transpose_z(j):
                pe.wait_ge(z_done, BT * j + BT)
                if not isinstance(j, int):
                    pe.wait_ge(zlo_done, C * j)
                for c in range(C):
                    for t in range(BT):
                        r = pe.transpose(pj[c][:, t * P:(t + 1) * P], z[:, t, c * P:(c + 1) * P], ident[:])
                    r.then_inc(tz_done, 1)

            def project(s, bank, col):
                b = bass.ds((s % BATCH) * SEQ, SEQ)
                w = slice(col, col + HD)
                for c in range(C):
                    pe.matmul(bank, wqkv[0][:, c, w], zh[:, c, b], start=(c == 0), stop=False)
                    pe.matmul(bank, wqkv[0][:, c, w], zl[:, c, b], start=False, stop=False)
                    r = pe.matmul(bank, wqkv[1][:, c, w], zh[:, c, b], start=False, stop=(c == C - 1))
                r.then_inc(pj_ready, 1)

            def key(s):
                pe.wait_ge(wqkv_in, 32 * (s // BATCH) + 32)
                project(s, pj[0][:], G * HD)

            def query(s, h):
                r = h + 1
                if r >= 2:
                    prev = r - 2 if r == 2 else r - 1
                    pe.wait_ge(raw_done, NR * s + prev + 1)
                project(s, pj[0 if h else 1][:], h * HD)

            def value(s):
                pe.wait_ge(raw_done, NR * s + 2)
                project(s, pj[1][:], (G + 1) * HD)

            def value_T(s):
                pe.wait_ge(vt_done, s + 1)
                for t in range(BT):
                    r = pe.transpose(pj[1][:, t * P:(t + 1) * P], vT[:, t * P:(t + 1) * P], ident[:])
                r.then_inc(pj_ready, 1)

            def scores(n, s, h):
                pe.wait_ge(ql_done, NR * s + h + 2)
                for i in QT:
                    bank, col = PLACE[i]
                    if col == 0 and not (isinstance(n, int) and n == 0):
                        pe.wait_ge(mx_done, BT * (n - 1) + (1, 3, 4)[bank])
                    w = (i + 1) * P
                    o, q = sc[bank][:, col:col + w], slice(i * P, (i + 1) * P)
                    pe.matmul(o, qh[:, h + 1, q], qh[:, 0, 0:w], start=True, stop=False)
                    pe.matmul(o, qh[:, h + 1, q], ql[:, 0, 0:w], start=False, stop=False)
                    r = pe.matmul(o, ql[:, h + 1, q], qh[:, 0, 0:w], start=False, stop=True)
                    if i != 2:
                        r.then_inc(sc_ready, 1)

            def transpose_p(s, h, fills):
                for k in fills:
                    q = 3 * G * s + 3 * h + k
                    if k == 0:
                        pe.wait_ge(nm_done, BT * (G * s + h) + BT)
                    pe.wait_ge(lo_done, q + 1)
                    for kt, col, _ in FILL[k]:
                        for i in range(kt, BT):
                            r = pe.transpose(pt[(3 * h + k) % 2][:, col + (i - kt) * P:col + (i - kt + 1) * P],
                                             pr[h % 2][:, OFF[i] + kt * P:OFF[i] + (kt + 1) * P], ident[:])
                    r.then_inc(pt_ready, 1)

            def weigh(s, h):
                pe.wait_ge(ol_done, G * s + h + 1)
                if h == 0:
                    pe.wait_ge(vl_done, s + 1)
                for k in range(3):
                    pe.wait_ge(lo_done, LO0 + 3 * G * s + 3 * h + k + 1)
                    for kt, col, w in FILL[k]:
                        o = o_ps[:, kt * P:SEQ]
                        a = slice(FCOL[k] + col, FCOL[k] + col + w)
                        end = k == 2
                        pe.matmul(o, vh[:, kt, :], pth[:, a], start=(kt == 0), stop=False)
                        pe.matmul(o, vh[:, kt, :], ptl[:, a], start=False, stop=False)
                        r = pe.matmul(o, vl[:, kt, :], pth[:, a], start=False, stop=end)
                r.then_inc(o_ready, 1)

            def output(s, u, last):
                if u == 0:
                    pe.wait_ge(wo_in, 32 * (s // BATCH) + 32)
                    pe.wait_ge(ol_done, OL0 + G * s + G)
                    if not last:
                        pe.wait_ge(vl_done, s + 2)
                elif not last:
                    pe.wait_ge(raw_done, NR * (s + 1) + NR)
                for t in range(2):
                    tok = slice((2 * u + t) * P, (2 * u + t + 1) * P)
                    o = pj[1 - u][:, t * D:(t + 1) * D]
                    for h in range(G):
                        pe.matmul(o, oh[:, h, tok], wo[0][:, h, :], start=(h == 0), stop=False)
                        pe.matmul(o, oh[:, h, tok], wo[1][:, h, :], start=False, stop=False)
                        r = pe.matmul(o, ol[:, h, tok], wo[0][:, h, :], start=False, stop=(h == G - 1))
                r.then_inc(pj_ready, 1)

            def step(s, last):
                n = G * s
                transpose_p(s, 0, (0, 1))
                scores(n + 2, s, 2)
                transpose_p(s, 0, (2,))
                weigh(s, 0)
                transpose_p(s, 1, (0, 1))
                scores(n + 3, s, 3)
                transpose_p(s, 1, (2,))
                weigh(s, 1)
                if not last:
                    key(s + 1)
                transpose_p(s, 2, (0, 1))
                if not last:
                    query(s + 1, 0)
                transpose_p(s, 2, (2,))
                weigh(s, 2)
                if not last:
                    query(s + 1, 1)
                    value(s + 1)
                transpose_p(s, 3, (0, 1))
                if not last:
                    scores(n + 4, s + 1, 0)
                transpose_p(s, 3, (2,))
                weigh(s, 3)
                if not last:
                    query(s + 1, 2)
                    value_T(s + 1)
                    scores(n + 5, s + 1, 1)
                    query(s + 1, 3)
                output(s, 0, last)
                output(s, 1, last)

            transpose_z(0)
            with pe.Fori(1, BATCH) as j:
                transpose_z(j)
            pe.wait_ge(zlo_done, C * BATCH)
            key(0)
            query(0, 0)
            query(0, 1)
            value(0)
            scores(0, 0, 0)
            query(0, 2)
            value_T(0)
            scores(1, 0, 1)
            query(0, 3)
            with pe.Fori(0, STEPS - 1) as s:
                step(s, False)
            step(STEPS - 1, True)


def macaron_kernel(nc, d, out):
    with ExitStack() as ctx:
        x = ctx.enter_context(nc.sbuf_tensor("x", [P, TILES, D], F32))
        ident = ctx.enter_context(nc.sbuf_tensor("ident", [P, P], F32))
        split = nc.dram_tensor("attn_split", [KV, 2, P, GW], F32, kind="Internal").ap()
        ffn_phase(nc, "f1", d, x, ident, True, split, None)
        attention_phase(nc, d, x, ident, split)
        ffn_phase(nc, "f2", d, x, ident, False, None, out)


def shape_constants():
    half = HD // 2
    freq = (1.0 / np.float32(ROPE_BASE) ** (np.arange(half, dtype=np.float32) / np.float32(half))).astype(np.float32)
    ang = np.arange(SEQ, dtype=np.float32)[None, :] * freq[:, None]
    cos, sin = np.cos(ang).astype(np.float32), np.sin(ang).astype(np.float32)
    mask = np.zeros((P, SEQ), np.float32)
    mask[:, SEQ - P:] = np.triu(np.full((P, P), BIG, np.float32), 1)
    pick = np.zeros((2 * E, E, P), np.float32)
    for e in range(E):
        pick[e, e] = pick[E + e, e] = 1.0
    return {
        "ident": np.eye(P, dtype=np.float32),
        "iota": np.arange(E, dtype=np.float32),
        "mask": mask,
        "pick": pick.reshape(2 * E, E * P),
        "rope_cos": np.concatenate([cos, cos]),
        "rope_sin": np.concatenate([-sin, sin]),
    }


def kernel(**inputs):
    import concourse.bacc as _bacc
    from concourse.bass_utils import run_bass_kernel_spmd as _run

    a = {k: np.asarray(v) for k, v in inputs.items()}
    wq, wk, wv, wo = (a[f"L0_attn_{n}"] for n in ("wq", "wk", "wv", "wo"))
    groups = []
    for g in range(KV):
        rows = np.concatenate([wq[g * G * HD:(g + 1) * G * HD], wk[g * HD:(g + 1) * HD], wv[g * HD:(g + 1) * HD]])
        qkv = rows.T.reshape(C, P, QKV).transpose(1, 0, 2).reshape(P, C * QKV)
        og = wo[:, g * G * HD:(g + 1) * G * HD].T.reshape(G, HD, D).transpose(1, 0, 2).reshape(P, G * D)
        groups.append(np.concatenate([qkv, og], axis=1))
    arrays = {
        "x": a["L0_attn_x"].reshape(TOKENS, D),
        "attn_w": np.stack(groups),
        "key_weights": a["L0_attn_key_weights"],
        "router_w": a["L0_ffn_router_w"].reshape(C, P, E).transpose(1, 0, 2),
        "router_b": a["L0_ffn_router_b"],
        "expert_w": a["L0_ffn_expert_w"].reshape(E, C, P, D).transpose(0, 2, 1, 3).reshape(E, P, C * D),
        "expert_b": a["L0_ffn_expert_b"].reshape(E * C, P).T,
        "proj_w": a["L0_ffn_proj_w"].reshape(C, P, D).transpose(1, 0, 2),
        "proj_b": a["L0_ffn_proj_b"],
        "norm_w": a["L0_ffn_norm_w"],
        **shape_constants(),
    }
    arrays = {k: np.ascontiguousarray(v) for k, v in arrays.items()}
    nc = _bacc.Bacc("TRN2", target_bir_lowering=False, num_devices=1)
    d = {k: nc.dram_tensor(f"in_{k}", v.shape, mybir.dt.from_np(v.dtype), kind="ExternalInput").ap() for k, v in arrays.items()}
    out = nc.dram_tensor("out_x", (TOKENS, D), F32, kind="ExternalOutput").ap()
    macaron_kernel(nc, d, out)
    r = _run(nc, [{f"in_{k}": v for k, v in arrays.items()}], core_ids=[0])
    return r.results[0]["out_x"].reshape(a["L0_attn_x"].shape)
```

```python
from contextlib import ExitStack

import numpy as np

import concourse.bass as bass
from concourse import mybir

F32 = mybir.dt.float32
F32R = mybir.dt.float32r
U32 = mybir.dt.uint32
ALU = mybir.AluOpType
ACT = mybir.ActivationFunctionType

P = 128
D = 256
C = D // P
BATCH, SEQ = 4, 512
TOKENS = BATCH * SEQ
TILES = TOKENS // P
BT = SEQ // P
HEADS, KV, HD = 16, 4, 128
G = HEADS // KV
E = 8
LN_EPS = 1e-5
RMS_EPS = 1e-6
QKV = (G + 2) * HD
GW = C * QKV + G * D
BIG = 1e30
ROPE_BASE = 10000.0


def layer_norm_block(dve, x, j, st, mv, ve, rs, z, ln_stats, ln_aggr, ln_var, rstd_done, z_done, passed):
    for t in range(BT):
        dve.bn_stats(st[:, t, :], x[:, bass.ds(j * BT + t, 1), :]).then_inc(ln_stats, 1)
    dve.wait_ge(ln_stats, j * BT + BT).then_inc(passed, 1)
    for t in range(BT):
        dve.bn_aggr(mv[:, t, :], st[:, t, :]).then_inc(ln_aggr, 1)
    dve.wait_ge(ln_aggr, j * BT + BT)
    dve.tensor_scalar(ve[:], mv[:, :, 1], LN_EPS, None, ALU.add).then_inc(ln_var, 1)
    dve.wait_ge(rstd_done, j + 1)
    for t in range(BT):
        dve.tensor_scalar(z[:, t, :], x[:, bass.ds(j * BT + t, 1), :], mv[:, t, 0:1], rs[:, t:t + 1],
                          ALU.subtract, ALU.mult).then_inc(z_done, 1)


def ffn_phase(nc, tag, d, x, ident, first, split, out):
    with ExitStack() as ctx:
        def sb(name, shape, dt=F32):
            return ctx.enter_context(nc.sbuf_tensor(f"{tag}_{name}", shape, dt))

        def ps(name, shape):
            return ctx.enter_context(nc.psum_tensor(f"{tag}_{name}", shape, F32))

        def sem(name):
            return ctx.enter_context(nc.semaphore(f"{tag}_{name}"))

        e_raw = sb("e_raw", [P, E, C * D])
        e_hi, e_lo = sb("e_hi", [P, E, C * D], F32R), sb("e_lo", [P, E, C * D], F32R)
        p_raw = sb("p_raw", [P, C, D])
        p_hi, p_lo = sb("p_hi", [P, C, D], F32R), sb("p_lo", [P, C, D], F32R)
        r_raw = sb("r_raw", [P, C, E])
        r_hl = sb("r_hl", [P, C, P], F32R)
        r_h0 = sb("r_h0", [P, C, P], F32R)
        e_bias = sb("e_bias", [P, E * C])
        p_bias, n_w, r_bias = sb("p_bias", [P, D]), sb("n_w", [P, D]), sb("r_bias", [P, E])
        iota = sb("iota", [P, E])
        pick = sb("pick", [2 * E, E * P])
        pick_r = sb("pick_r", [2 * E, E, P], F32R)
        st, mv, ve, rs = sb("st", [P, BT, 6]), sb("mv", [P, BT, 2]), sb("ve", [P, BT]), sb("rs", [P, BT])
        mhalf = sb("mhalf", [P, BT])
        z = sb("z", [P, BT, D])
        zh, zl = sb("zh", [P, 2 * C, SEQ], F32R), sb("zl", [P, 2 * C, SEQ], F32R)
        zres = sb("zres", [P, 2 * BT, D])
        rT = sb("rT", [2 * E, SEQ])
        l0, lg = sb("l0", [P, BT, E]), sb("lg", [P, BT, E])
        top, topi = sb("top", [P, BT, 8]), sb("topi", [P, BT, 8], U32)
        topf = sb("topf", [P, BT, 2])
        gap, th = sb("gap", [P, BT]), sb("th", [P, BT])
        w0, w1 = sb("w0", [P, BT]), sb("w1", [P, BT])
        oh0, oh1 = sb("oh0", [P, BT, E]), sb("oh1", [P, BT, E])
        full = sb("full", [P, BT, E])
        full_hi = sb("full_hi", [P, BT, E], F32R)
        fw = sb("fw", [P, BT, P])
        wT = sb("wT", [2 * E, SEQ], F32R)
        s_ring = [sb(f"s{n}", [P, SEQ]) for n in range(4)]
        u_ring = [sb(f"u{n}", [P, SEQ]) for n in range(4)]
        acc = sb("acc", [P, C, SEQ])
        ch, cl = sb("ch", [P, C, SEQ], F32R), sb("cl", [P, C, SEQ], F32R)
        y, sq = sb("y", [P, BT, D]), sb("sq", [P, BT, D])
        ss, ms, rr = sb("ss", [P, BT]), sb("ms", [P, BT]), sb("rr", [P, BT])
        if first:
            kw = sb("kw", [P, HEADS])
            a_raw = sb("a_raw", [P, GW])
            a_hi, a_lo = sb("a_hi", [P, GW], F32R), sb("a_lo", [P, GW], F32R)

        ex_ps = [ps(f"ex{n}", [P, SEQ]) for n in range(4)]
        wb_ps = ps("wb", [P, SEQ])
        y_ps = ps("y_ps", [P, SEQ])
        t_ps = [ps(f"t{n}", [P, SEQ]) for n in range(2)]

        x_in = [sem(f"x_in{n}") for n in range(BATCH)]
        e_in = [sem(f"e_in{n}") for n in range(E)]
        small_in, pr_in = sem("small_in"), sem("pr_in")
        e_hi_done, e_lo_done, pr_split, setup, consts = (sem(n) for n in ("e_hi_done", "e_lo_done", "pr_split", "setup", "consts"))
        ln_stats, ln_aggr, ln_var, rstd_done, z_done = (sem(n) for n in ("ln_stats", "ln_aggr", "ln_var", "rstd_done", "z_done"))
        half_set = sem("half_set")
        passed = sem("passed")
        tz_done, zhi_done, zlo_done, zres_done = (sem(n) for n in ("tz_done", "zhi_done", "zlo_done", "zres_done"))
        rout_done, rT_done, tb_done, gate, tanh_done = (sem(n) for n in ("rout_done", "rT_done", "tb_done", "gate", "tanh_done"))
        gap_done, fw_done, tw_done, wT_done = (sem(n) for n in ("gap_done", "fw_done", "tw_done", "wT_done"))
        ex_done, silu_done, sel_done, mult_done, acc_done = (sem(n) for n in ("ex_done", "silu_done", "sel_done", "mult_done", "acc_done"))
        chi_done, clo_done, y_done, yadd_done, sq_done = (sem(n) for n in ("chi_done", "clo_done", "y_done", "yadd_done", "sq_done"))
        rms, rr_done, xn_done, x_done, out_done = (sem(n) for n in ("rms", "rr_done", "xn_done", "x_done", "out_done"))
        if first:
            a_in, a_scaled, a_hi_done, a_lo_done, a_out = (sem(n) for n in ("a_in", "a_scaled", "a_hi_done", "a_lo_done", "a_out"))

        RING = len(ex_ps)
        SILU0 = RING
        MULT0 = len(s_ring)
        YADD0 = 2
        X0 = 1
        GATE = 20
        EW = C * D

        block = ctx.enter_context(nc.Block())

        @block.sync
        def _(sp):
            if first:
                xr = d["x"].rearrange("(b t p) d -> b p t d", t=BT, p=P)
                for b in range(BATCH):
                    if b == 0:
                        sp.dma_start(x[:, 0:BT, :], xr[0]).then_inc(x_in[0], 16)
                        sp.dma_start(r_raw[:], d["router_w"]).then_inc(pr_in, 16)
                        sp.dma_start(p_raw[:], d["proj_w"]).then_inc(pr_in, 16)
                        for e in range(E):
                            sp.dma_start(e_raw[:, e, :], d["expert_w"][e]).then_inc(e_in[e], 16)
                    else:
                        sp.dma_start(x[:, b * BT:(b + 1) * BT, :], xr[b]).then_inc(x_in[b], 16)
            else:
                sp.dma_start(r_raw[:], d["router_w"]).then_inc(pr_in, 16)
                sp.dma_start(p_raw[:], d["proj_w"]).then_inc(pr_in, 16)
                for e in range(E):
                    sp.dma_start(e_raw[:, e, :], d["expert_w"][e]).then_inc(e_in[e], 16)

            def block_io(i):
                if first:
                    sp.dma_start(a_raw[:], d["attn_w"][bass.ds(i, 1)].rearrange("o p n -> (o p) n")).then_inc(a_in, 16)
                    sp.wait_ge(a_lo_done, i + 1).then_inc(passed, 1)
                    sp.dma_start(split[bass.ds(i, 1), 0].rearrange("o p n -> (o p) n"), a_hi[:].bitcast(F32)).then_inc(a_out, 16)
                    sp.dma_start(split[bass.ds(i, 1), 1].rearrange("o p n -> (o p) n"), a_lo[:].bitcast(F32)).then_inc(a_out, 16)
                    sp.wait_ge(a_out, 32 * i + 32).then_inc(passed, 1)
                if out is not None:
                    sp.wait_ge(x_done, X0 + i + 1).then_inc(passed, 1)
                    sp.dma_start(out.rearrange("(b t p) d -> b p t d", t=BT, p=P)[bass.ds(i, 1)].rearrange("o p t d -> (o p) t d"),
                                 x[:, bass.ds(i * BT, BT), :]).then_inc(out_done, 16)

            with sp.Fori(0, BATCH) as i:
                block_io(i)
            if out is not None:
                sp.wait_ge(out_done, 16 * BATCH)

        @block.gpsimd
        def _(pool):
            pool.sem_inc(x_done, X0)
            pool.memset(mhalf[:], -0.5).then_inc(half_set, 1)
            pool.dma_start(p_bias[:], d["proj_b"].partition_broadcast(P)).then_inc(small_in, 16)
            pool.dma_start(n_w[:], d["norm_w"].partition_broadcast(P)).then_inc(small_in, 16)
            pool.dma_start(r_bias[:], d["router_b"].partition_broadcast(P)).then_inc(small_in, 16)
            pool.dma_start(iota[:], d["iota"].partition_broadcast(P)).then_inc(small_in, 16)
            pool.dma_start(e_bias[:], d["expert_b"]).then_inc(small_in, 16)
            pool.dma_start(pick[:], d["pick"]).then_inc(small_in, 16)
            if first:
                pool.dma_start(ident[:], d["ident"]).then_inc(small_in, 16)
                pool.dma_start(kw[:], d["key_weights"].partition_broadcast(P)).then_inc(small_in, 16)
            pool.wait_ge(small_in, 16 * (8 if first else 6))

            def rstd(j):
                pool.wait_ge(ln_var, j + 1)
                pool.tensor_tensor(rs[:], ve[:], mhalf[:], ALU.pow).then_inc(rstd_done, 1)

            def residual(j):
                pool.wait_ge(z_done, BT * j + BT)
                pool.tensor_tensor(zres[:, bass.ds((j % 2) * BT, BT), :], z[:],
                                   p_bias[:].unsqueeze(1).to_broadcast([P, BT, D]), ALU.add).then_inc(zres_done, 1)

            def body(i, more):
                if more:
                    rstd(i + 1)
                if first:
                    pool.wait_ge(consts, 2)
                    pool.wait_ge(a_in, 16 * i + 16)
                    for c in range(C):
                        q = a_raw[:, c * QKV + HD:c * QKV + QKV - HD].rearrange("p (h d) -> p h d", h=G)
                        pool.tensor_tensor(q, q, kw[:, bass.ds(i * G, G)].unsqueeze(2).to_broadcast([P, G, HD]),
                                           ALU.mult).then_inc(a_scaled, 1)
                for e in range(1, E):
                    for f in range(C):
                        n = C * e + f
                        pool.wait_ge(mult_done, MULT0 + 2 * E * i + n + 1)
                        if e > 1:
                            pool.wait_ge(acc_done, 2 * (E - 1) * i + 2 * (e - 2) + f + 1)
                        pool.tensor_tensor(acc[:, f, :], acc[:, f, :], u_ring[n % 4][:], ALU.add).then_inc(acc_done, 1)
                    if e == 1 and more:
                        residual(i + 1)
                pool.wait_ge(rms, i + 1)
                pool.tensor_tensor(rr[:], ms[:], mhalf[:], ALU.pow).then_inc(rr_done, 1)
                pool.wait_ge(xn_done, BT * i + BT)
                xb = x[:, bass.ds(i * BT, BT), :]
                pool.tensor_tensor(xb, xb, y[:], ALU.add).then_inc(x_done, 1)

            pool.wait_ge(half_set, 1)
            rstd(0)
            residual(0)
            with pool.Fori(0, BATCH - 1) as i:
                body(i, True)
            body(BATCH - 1, False)

        @block.vector
        def _(dve):
            dve.sem_inc(mult_done, MULT0)
            dve.sem_inc(yadd_done, YADD0)
            dve.memset(fw[:], 0.0).then_inc(setup, 1)
            dve.memset(r_hl[:].bitcast(F32), 0.0).then_inc(setup, 1)
            dve.memset(r_h0[:].bitcast(F32), 0.0).then_inc(setup, 1)

            def norm(j):
                layer_norm_block(dve, x, j, st, mv, ve, rs, z, ln_stats, ln_aggr, ln_var, rstd_done, z_done, passed)

            def z_rest(j):
                for c in range(C):
                    dve.wait_ge(zhi_done, C * j + c + 1)
                    k = bass.ds((j % 2) * C + c, 1)
                    dve.tensor_tensor(zl[:, k, :], t_ps[c][:].unsqueeze(1), zh[:, k, :].bitcast(F32),
                                      ALU.subtract).then_inc(zlo_done, 1)

            def gating(j):
                g = GATE * j
                lp = t_ps[1][:, 0:BT * 2 * E].rearrange("p (t k) -> p t k", t=BT)
                dve.wait_ge(tb_done, j + 1)
                dve.tensor_tensor(l0[:], lp[:, :, E:2 * E], r_bias[:].unsqueeze(1).to_broadcast([P, BT, E]),
                                  ALU.add).then_inc(gate, 1)
                dve.wait_ge(gate, g + 1)
                dve.tensor_tensor(lg[:], lp[:, :, 0:E], l0[:], ALU.add).then_inc(gate, 1)
                dve.wait_ge(gate, g + 2).then_inc(passed, 1)
                for t in range(BT):
                    dve.max(top[:, t, :], lg[:, t, :]).then_inc(gate, 1)
                dve.wait_ge(gate, g + 6)
                dve.tensor_tensor(gap[:].unsqueeze(2), top[:, :, 0:1], top[:, :, 1:2], ALU.subtract).then_inc(gap_done, 1)
                for t in range(BT):
                    dve.max_index(topi[:, t, :], top[:, t, :], lg[:, t, :]).then_inc(gate, 1)
                dve.wait_ge(gate, g + 10)
                dve.tensor_copy(topf[:], topi[:, :, 0:2]).then_inc(gate, 1)
                dve.wait_ge(gate, g + 11)
                io = iota[:].unsqueeze(1).to_broadcast([P, BT, E])
                dve.tensor_tensor(oh0[:], io, topf[:, :, 0:1].to_broadcast([P, BT, E]), ALU.is_equal).then_inc(gate, 1)
                dve.tensor_tensor(oh1[:], io, topf[:, :, 1:2].to_broadcast([P, BT, E]), ALU.is_equal).then_inc(gate, 1)
                dve.wait_ge(tanh_done, j + 1)
                dve.tensor_scalar(w0[:], th[:], 0.5, 0.5, ALU.mult, ALU.add).then_inc(gate, 1)
                dve.tensor_scalar(w1[:], th[:], -0.5, 0.5, ALU.mult, ALU.add).then_inc(gate, 1)
                dve.wait_ge(gate, g + 15)
                dve.tensor_tensor(oh0[:], oh0[:], w0[:].unsqueeze(2).to_broadcast([P, BT, E]), ALU.mult).then_inc(gate, 1)
                dve.tensor_tensor(oh1[:], oh1[:], w1[:].unsqueeze(2).to_broadcast([P, BT, E]), ALU.mult).then_inc(gate, 1)
                dve.wait_ge(gate, g + 17)
                dve.tensor_tensor(full[:], oh0[:], oh1[:], ALU.add).then_inc(gate, 1)
                dve.wait_ge(gate, g + 18)
                dve.tensor_copy(full_hi[:], full[:]).then_inc(gate, 1)
                dve.wait_ge(gate, g + 19)
                dve.tensor_copy(fw[:, :, 0:E], full_hi[:].bitcast(F32)).then_inc(gate, 1)
                dve.tensor_tensor(fw[:, :, E:2 * E], full[:], full_hi[:].bitcast(F32), ALU.subtract).then_inc(fw_done, 1)

            def body(i, more):
                if more:
                    dve.wait_ge(zres_done, i + 1)
                    norm(i + 1)
                for e in range(E):
                    for f in range(C):
                        n = C * e + f
                        dve.wait_ge(silu_done, SILU0 + 2 * E * i + n + 1)
                        if f == 0:
                            dve.wait_ge(sel_done, E * i + e + 1)
                        if e >= 3:
                            dve.wait_ge(acc_done, 2 * (E - 1) * i + 2 * (e - 3) + f + 1)
                        to = acc[:, f, :] if e == 0 else u_ring[n % 4][:]
                        dve.tensor_tensor(to, s_ring[n % 4][:], wb_ps[:], ALU.mult).then_inc(mult_done, 1)
                    if first and e == 1:
                        for half in range(2):
                            cols = slice(half * GW // 2, (half + 1) * GW // 2)
                            dve.wait_ge(a_hi_done, 2 * i + half + 1)
                            r = dve.tensor_tensor(a_lo[:, cols], a_raw[:, cols], a_hi[:, cols].bitcast(F32), ALU.subtract)
                        r.then_inc(a_lo_done, 1)
                    if more and e == 3:
                        z_rest(i + 1)
                    if more and e == 6:
                        gating(i + 1)
                for f in range(C):
                    dve.wait_ge(chi_done, C * i + f + 1)
                    dve.tensor_tensor(cl[:, f, :], acc[:, f, :], ch[:, f, :].bitcast(F32), ALU.subtract).then_inc(clo_done, 1)
                dve.wait_ge(x_done, X0 + i)
                dve.wait_ge(zres_done, i + 1)
                for u in range(2):
                    dve.wait_ge(y_done, 2 * i + u + 1)
                    src = (y_ps, wb_ps)[u][:].rearrange("p (t d) -> p t d", t=2)
                    dve.tensor_tensor(y[:, 2 * u:2 * u + 2, :], src, zres[:, bass.ds((i % 2) * BT + 2 * u, 2), :],
                                      ALU.add).then_inc(yadd_done, 1)
                dve.wait_ge(sq_done, BT * i + BT)
                dve.tensor_scalar(ms[:], ss[:], 1.0 / D, RMS_EPS, ALU.mult, ALU.add).then_inc(rms, 1)
                dve.wait_ge(rr_done, i + 1)
                for t in range(BT):
                    dve.scalar_tensor_tensor(out=y[:, t, :], in0=y[:, t, :], scalar=rr[:, t:t + 1], in1=n_w[:],
                                             op0=ALU.mult, op1=ALU.mult).then_inc(xn_done, 1)

            if first:
                dve.wait_ge(x_in[0], 16)
            norm(0)
            dve.wait_ge(small_in, 16 * (8 if first else 6))
            dve.wait_ge(setup, 3)
            dve.tensor_scalar(n_w[:], n_w[:], 0.5, None, ALU.mult).then_inc(consts, 1)
            if first:
                dve.tensor_scalar(kw[:], kw[:], -float(HD) ** -0.5, None, ALU.mult).then_inc(consts, 1)
            dve.tensor_copy(pick_r[:].rearrange("k e p -> k (e p)"), pick[:]).then_inc(setup, 1)
            dve.wait_ge(pr_in, 32)
            dve.tensor_copy(r_hl[:, :, 0:E], r_raw[:]).then_inc(pr_split, 1)
            dve.tensor_copy(r_h0[:, :, 0:E], r_raw[:]).then_inc(pr_split, 1)
            dve.wait_ge(pr_split, 2)
            dve.tensor_tensor(r_hl[:, :, E:2 * E], r_raw[:], r_hl[:, :, 0:E].bitcast(F32), ALU.subtract).then_inc(pr_split, 1)
            z_rest(0)
            for e in range(E):
                dve.wait_ge(e_hi_done, e + 1)
                dve.tensor_tensor(e_lo[:, e, :], e_raw[:, e, :], e_hi[:, e, :].bitcast(F32), ALU.subtract).then_inc(e_lo_done, 1)
                if e == 3:
                    gating(0)
            dve.wait_ge(e_hi_done, E + 1)
            dve.tensor_tensor(p_lo[:], p_raw[:], p_hi[:].bitcast(F32), ALU.subtract).then_inc(pr_split, 1)
            if first:
                for b in range(1, BATCH):
                    dve.wait_ge(x_in[b], 16)
            with dve.Fori(0, BATCH - 1) as i:
                body(i, True)
            body(BATCH - 1, False)

        @block.scalar
        def _(act):
            act.sem_inc(silu_done, SILU0)

            def z_lead(j):
                for c in range(C):
                    act.wait_ge(tz_done, C * j + c + 1)
                    act.activation(zh[:, bass.ds((j % 2) * C + c, 1), :], t_ps[c][:].unsqueeze(1),
                                   ACT.Copy).then_inc(zhi_done, 1)

            def logits_out(j):
                act.wait_ge(rout_done, j + 1)
                act.activation(rT[:], t_ps[0][0:2 * E, :], ACT.Copy).then_inc(rT_done, 1)

            def half_tanh(j):
                act.wait_ge(gap_done, j + 1)
                act.activation(th[:], gap[:], ACT.Tanh, scale=0.5).then_inc(tanh_done, 1)

            def weights_out(j):
                act.wait_ge(tw_done, j + 1)
                act.activation(wT[:], t_ps[0][0:2 * E, :], ACT.Copy).then_inc(wT_done, 1)

            def body(i, more):
                for e in range(E):
                    for f in range(C):
                        n = C * e + f
                        act.wait_ge(ex_done, 2 * E * i + n + 1)
                        act.wait_ge(mult_done, 2 * E * i + n + 1)
                        act.activation(s_ring[n % 4][:], ex_ps[n % RING][:], ACT.Silu,
                                       bias=e_bias[:, n:n + 1]).then_inc(silu_done, 1)
                    if first and e == 0:
                        act.wait_ge(a_scaled, 2 * i + 2)
                        for half in range(2):
                            cols = slice(half * GW // 2, (half + 1) * GW // 2)
                            act.activation(a_hi[:, cols], a_raw[:, cols], ACT.Copy).then_inc(a_hi_done, 1)
                    if more and e == 2:
                        z_lead(i + 1)
                    if more and e == 4:
                        logits_out(i + 1)
                    if more and e == 6:
                        half_tanh(i + 1)
                for f in range(C):
                    act.wait_ge(acc_done, 2 * (E - 1) * i + 2 * (E - 2) + f + 1)
                    act.activation(ch[:, f, :], acc[:, f, :], ACT.Copy).then_inc(chi_done, 1)
                if more:
                    weights_out(i + 1)
                for t in range(BT):
                    act.wait_ge(yadd_done, YADD0 + 2 * i + t // 2 + 1)
                    act.activation(sq[:, t, :], y[:, t, :], ACT.Square, accum_out=ss[:, t:t + 1]).then_inc(sq_done, 1)

            z_lead(0)
            for e in range(2):
                act.wait_ge(e_in[e], 16)
                act.activation(e_hi[:, e, :], e_raw[:, e, :], ACT.Copy).then_inc(e_hi_done, 1)
            logits_out(0)
            for e in range(2, 4):
                act.wait_ge(e_in[e], 16)
                act.activation(e_hi[:, e, :], e_raw[:, e, :], ACT.Copy).then_inc(e_hi_done, 1)
            half_tanh(0)
            for e in range(4, E):
                act.wait_ge(e_in[e], 16)
                act.activation(e_hi[:, e, :], e_raw[:, e, :], ACT.Copy).then_inc(e_hi_done, 1)
            act.wait_ge(pr_in, 32)
            act.activation(p_hi[:], p_raw[:], ACT.Copy).then_inc(e_hi_done, 1)
            weights_out(0)
            act.wait_ge(small_in, 16 * (8 if first else 6))
            with act.Fori(0, BATCH - 1) as i:
                body(i, True)
            body(BATCH - 1, False)

        @block.tensor
        def _(pe):
            def transpose_z(j):
                pe.wait_ge(z_done, BT * j + BT)
                for c in range(C):
                    for t in range(BT):
                        r = pe.transpose(t_ps[c][:, t * P:(t + 1) * P], z[:, t, c * P:(c + 1) * P], ident[:])
                    r.then_inc(tz_done, 1)

            def router(j):
                pe.wait_ge(zlo_done, C * j + C)
                for c in range(C):
                    k = bass.ds((j % 2) * C + c, 1)
                    pe.matmul(t_ps[0][:], r_hl[:, c, :], zh[:, k, :].rearrange("p o s -> p (o s)"), start=(c == 0), stop=False)
                    r = pe.matmul(t_ps[0][:], r_h0[:, c, :], zl[:, k, :].rearrange("p o s -> p (o s)"), start=False, stop=(c == C - 1))
                r.then_inc(rout_done, 1)

            def logits_back(j):
                pe.wait_ge(rT_done, j + 1).then_inc(passed, 1)
                for t in range(BT):
                    r = pe.transpose(t_ps[1][:, t * 2 * E:(t + 1) * 2 * E], rT[:, t * P:(t + 1) * P], ident[0:2 * E, 0:2 * E])
                r.then_inc(tb_done, 1)

            def weights_T(j):
                pe.wait_ge(fw_done, j + 1)
                for t in range(BT):
                    r = pe.transpose(t_ps[0][:, t * P:(t + 1) * P], fw[:, t, :], ident[:])
                r.then_inc(tw_done, 1)

            def body(i, more):
                for e in range(E):
                    for f in range(C):
                        n = C * e + f
                        pe.wait_ge(silu_done, 2 * E * i + n + 1)
                        bank = ex_ps[n % RING][:]
                        for c in range(C):
                            k = bass.ds((i % 2) * C + c, 1)
                            w = slice(c * D + f * P, c * D + (f + 1) * P)
                            h, l = (v[:, k, :].rearrange("p o s -> p (o s)") for v in (zh, zl))
                            pe.matmul(bank, e_hi[:, e, w], h, start=(c == 0), stop=False)
                            pe.matmul(bank, e_hi[:, e, w], l, start=False, stop=False)
                            r = pe.matmul(bank, e_lo[:, e, w], h, start=False, stop=(c == C - 1))
                        r.then_inc(ex_done, 1)
                    if e == 0:
                        pe.wait_ge(wT_done, i + 1)
                        pe.wait_ge(yadd_done, 2 * i + 2)
                    else:
                        pe.wait_ge(mult_done, MULT0 + 2 * E * i + C * e)
                    pe.matmul(wb_ps[:], pick_r[:, e, :], wT[:], start=True, stop=True).then_inc(sel_done, 1)
                    if more and e == 1:
                        transpose_z(i + 1)
                    if more and e == 3:
                        router(i + 1)
                    if more and e == 4:
                        logits_back(i + 1)
                if more:
                    weights_T(i + 1)
                pe.wait_ge(clo_done, C * i + C)
                for u in range(2):
                    bank = (y_ps, wb_ps)[u]
                    for t in range(2):
                        tok = slice((2 * u + t) * P, (2 * u + t + 1) * P)
                        o = bank[:, t * D:(t + 1) * D]
                        for f in range(C):
                            pe.matmul(o, ch[:, f, tok], p_hi[:, f, :], start=(f == 0), stop=False)
                            pe.matmul(o, ch[:, f, tok], p_lo[:, f, :], start=False, stop=False)
                            r = pe.matmul(o, cl[:, f, tok], p_hi[:, f, :], start=False, stop=(f == C - 1))
                    r.then_inc(y_done, 1)

            pe.wait_ge(small_in, 16 * (8 if first else 6))
            transpose_z(0)
            pe.wait_ge(setup, 4)
            pe.wait_ge(pr_split, 3)
            router(0)
            logits_back(0)
            weights_T(0)
            for e in range(E):
                pe.wait_ge(e_lo_done, e + 1)
            pe.wait_ge(pr_split, 4)
            with pe.Fori(0, BATCH - 1) as i:
                body(i, True)
            body(BATCH - 1, False)


def attention_phase(nc, d, x, ident, split):
    with ExitStack() as ctx:
        def sb(name, shape, dt=F32):
            return ctx.enter_context(nc.sbuf_tensor(f"at_{name}", shape, dt))

        def ps(name, shape):
            return ctx.enter_context(nc.psum_tensor(f"at_{name}", shape, F32))

        def sem(name):
            return ctx.enter_context(nc.semaphore(f"at_{name}"))

        STEPS = KV * BATCH
        NR = G + 1
        OFF = [P * (i * (i + 1) // 2) for i in range(BT)]
        TRI = OFF[-1] + BT * P
        QT = (3, 2, 0, 1)
        FILL = (((0, 0, 4 * P),), ((1, 0, 3 * P), (3, 3 * P, P)), ((2, 0, 2 * P),))
        NF = len(FILL)
        FCOL, FLEN = (0, SEQ, 2 * SEQ), (SEQ, SEQ, 2 * P)

        zh, zl = sb("zh", [P, C, TOKENS], F32R), sb("zl", [P, C, TOKENS], F32R)
        cosT, sinT, mask = sb("cos", [P, SEQ]), sb("sin", [P, SEQ]), sb("mask", [P, SEQ])
        st, mv, ve, rs = sb("st", [P, BT, 6]), sb("mv", [P, BT, 2]), sb("ve", [P, BT]), sb("rs", [P, BT])
        mhalf = sb("mhalf", [P, BT])
        z = sb("z", [P, BT, D])
        wqkv = [sb(f"wqkv{n}", [P, C, QKV], F32R) for n in range(2)]
        wo = [sb(f"wo{n}", [P, G, D], F32R) for n in range(2)]
        raw = [sb(f"raw{r}", [P, SEQ]) for r in range(NR)]
        swap = [sb(f"swap{r}", [P, SEQ]) for r in range(NR)]
        rot = [sb(f"rot{n}", [P, SEQ]) for n in range(2)]
        kh, kl = sb("kh", [P, 2, SEQ], F32R), sb("kl", [P, 2, SEQ], F32R)
        qh, ql = sb("qh", [P, G, SEQ], F32R), sb("ql", [P, G, SEQ], F32R)
        vT = sb("vT", [P, SEQ])
        vh, vl = sb("vh", [P, BT, HD], F32R), sb("vl", [P, BT, HD], F32R)
        sm = [sb(f"sm{n}", [P, TRI]) for n in range(2)]
        pr = [sb(f"pr{n}", [P, TRI]) for n in range(2)]
        low, tot, inv = ([sb(f"{n}{k}", [P, BT]) for k in range(2)] for n in ("low", "tot", "inv"))
        pth = [sb(f"pth{n}", [P, TRI], F32R) for n in range(2)]
        ptl = [sb(f"ptl{n}", [P, TRI], F32R) for n in range(2)]
        oh, ol = sb("oh", [P, G, SEQ], F32R), sb("ol", [P, G, SEQ], F32R)

        pj = [ps(f"pj{n}", [P, SEQ]) for n in range(2)]
        sc = [ps(f"sc{n}", [P, SEQ]) for n in range(3)]
        pt = [ps(f"pt{n}", [P, SEQ]) for n in range(2)]
        o_ps = ps("o", [P, SEQ])
        PLACE = {3: (0, 0), 2: (1, 0), 0: (1, 3 * P), 1: (2, 0)}

        const_in, wa_in, wb_in, wo_in = (sem(n) for n in ("const_in", "wa_in", "wb_in", "wo_in"))
        swap_in = [sem(f"swap_in{r}") for r in range(NR)]
        ln_stats, ln_aggr, ln_var, rstd_done, z_done = (sem(n) for n in ("ln_stats", "ln_aggr", "ln_var", "rstd_done", "z_done"))
        half_set = sem("half_set")
        passed = sem("passed")
        tz_done, zhi_done, zlo_done = (sem(n) for n in ("tz_done", "zhi_done", "zlo_done"))
        pj_ready, sc_ready, pt_ready, o_ready = (sem(n) for n in ("pj_ready", "sc_ready", "pt_ready", "o_ready"))
        raw_done, qh_done, vt_done, vh_done, vl_done = (sem(n) for n in ("raw_done", "qh_done", "vt_done", "vh_done", "vl_done"))
        ex_done, hi_done, lo_done, oh_done, ol_done = (sem(n) for n in ("ex_done", "hi_done", "lo_done", "oh_done", "ol_done"))
        mx_done, inv_done, nm_done, xu_done = (sem(n) for n in ("mx_done", "inv_done", "nm_done", "xu_done"))
        cos_done, sin_done, sum_done, ql_done = (sem(n) for n in ("cos_done", "sin_done", "sum_done", "ql_done"))

        LO0 = 2
        OL0 = 1
        K, Q0, Q1, V, Q2, VT, Q3 = range(7)
        OWN = 7
        BANK = {K: 1, Q0: 0, Q1: 1, V: 0, Q2: 1, VT: 0, Q3: 1}
        OUT_BANK = (1, 0)
        QFILL = (K, Q0, Q1, Q2, Q3)

        def proj_fill(s, k):
            if isinstance(s, int) and s < 2:
                return OWN * s + k + 1
            return 2 * OWN + (OWN + 2) * (s - 2) + k + 1 + (2 if k > Q0 else 0)

        def out_fill(s, u):
            if isinstance(s, int) and s >= STEPS - 2:
                return 2 * OWN + (OWN + 2) * (STEPS - 2) + 2 * (s - (STEPS - 2)) + u + 1
            return 2 * OWN + (OWN + 2) * s + 2 + u + 1

        block = ctx.enter_context(nc.Block())

        @block.sync
        def _(sp):
            def load_proj(g, cols, done):
                for n in range(2):
                    src = split[bass.ds(g, 1), n, :, 0:C * QKV].rearrange("o p (c n) -> (o p) c n", c=C)
                    sp.dma_start(wqkv[n][:, :, cols].bitcast(F32), src[:, :, cols]).then_inc(done, 16)

            def load_wo(g):
                for n in range(2):
                    sp.dma_start(wo[n][:].rearrange("p h n -> p (h n)").bitcast(F32),
                                 split[bass.ds(g, 1), n, :, C * QKV:GW].rearrange("o p n -> (o p) n")).then_inc(wo_in, 16)

            FIRST, LATER = slice(0, 2 * HD), slice(2 * HD, QKV)

            def swaps(s, new_wo=None, new_proj=None):
                for r in range(NR):
                    sp.wait_ge(raw_done, NR * s + r + 1).then_inc(passed, 1)
                    sp.dma_start(swap[r][0:HD // 2, :], raw[r][HD // 2:HD, :]).then_inc(swap_in[r], 16)
                    sp.dma_start(swap[r][HD // 2:HD, :], raw[r][0:HD // 2, :]).then_inc(swap_in[r], 16)
                    if r == 1 and new_proj is not None:
                        load_proj(new_proj, FIRST, wa_in)
                    if r == 2 and new_wo is not None:
                        load_wo(new_wo)
                    if r == NR - 1 and new_proj is not None:
                        load_proj(new_proj, LATER, wb_in)

            load_proj(0, FIRST, wa_in)
            sp.dma_start(cosT[:], d["rope_cos"]).then_inc(const_in, 16)
            sp.dma_start(sinT[:], d["rope_sin"]).then_inc(const_in, 16)
            load_proj(0, LATER, wb_in)
            sp.dma_start(mask[:], d["mask"]).then_inc(const_in, 16)
            load_wo(0)
            with sp.Fori(0, BATCH - 1) as s:
                swaps(s)
            swaps(BATCH - 1, new_proj=1)
            with sp.Fori(1, KV - 1) as g:
                swaps(BATCH * g)
                swaps(BATCH * g + 1, new_wo=g)
                swaps(BATCH * g + 2)
                swaps(BATCH * g + 3, new_proj=g + 1)
            last = BATCH * (KV - 1)
            swaps(last)
            swaps(last + 1, new_wo=KV - 1)
            with sp.Fori(last + 2, STEPS) as s:
                swaps(s)

        @block.gpsimd
        def _(pool):
            def rest(s, r):
                pool.wait_ge(qh_done, NR * s + r + 1)
                to, lead = ((kl, kh) if r == 0 else (ql, qh))
                k = bass.ds(s % 2, 1) if r == 0 else slice(r - 1, r)
                pool.tensor_tensor(to[:, k, :], rot[r % 2][:].unsqueeze(1), lead[:, k, :].bitcast(F32),
                                   ALU.subtract).then_inc(ql_done, 1)

            def rotate(s, r):
                if r >= 2:
                    pool.wait_ge(ql_done, NR * s + r - 1)
                elif not (isinstance(s, int) and s == 0):
                    pool.wait_ge(ql_done, NR * s)
                pool.wait_ge(raw_done, NR * s + r + 1)
                pool.tensor_tensor(rot[r % 2][:], raw[r][:], cosT[:], ALU.mult).then_inc(cos_done, 1)
                pool.wait_ge(swap_in[r], 32 * s + 32)
                pool.tensor_tensor(swap[r][:], swap[r][:], sinT[:], ALU.mult).then_inc(sin_done, 1)
                pool.wait_ge(sin_done, NR * s + r + 1)
                pool.tensor_tensor(rot[r % 2][:], rot[r % 2][:], swap[r][:], ALU.add).then_inc(sum_done, 1)

            def rstd(j):
                pool.wait_ge(ln_var, j + 1)
                pool.tensor_tensor(rs[:], ve[:], mhalf[:], ALU.pow).then_inc(rstd_done, 1)

            def rope(s):
                rotate(s, 0)
                for r in range(1, NR):
                    rest(s, r - 1)
                    rotate(s, r)

            pool.memset(mhalf[:], -0.5).then_inc(half_set, 1)
            pool.wait_ge(half_set, 1)
            rstd(0)
            with pool.Fori(1, BATCH) as j:
                rstd(j)
            pool.wait_ge(const_in, 48)
            rope(0)
            with pool.Fori(1, STEPS) as s:
                rest(s - 1, NR - 1)
                rope(s)
            rest(STEPS - 1, NR - 1)

        @block.vector
        def _(dve):
            dve.sem_inc(lo_done, LO0)
            dve.sem_inc(ol_done, OL0)

            def norm(j):
                layer_norm_block(dve, x, j, st, mv, ve, rs, z, ln_stats, ln_aggr, ln_var, rstd_done, z_done, passed)

            def z_rest(j):
                for c in range(C):
                    dve.wait_ge(zhi_done, C * j + c + 1)
                    cols = bass.ds(j * SEQ, SEQ)
                    dve.tensor_tensor(zl[:, c, cols], pj[c][:], zh[:, c, cols].bitcast(F32), ALU.subtract).then_inc(zlo_done, 1)

            def mask_min(n, h):
                for k, i in enumerate(QT):
                    bank, col = PLACE[i]
                    if k == 0 and not (isinstance(n, int) and n < 2):
                        dve.wait_ge(ex_done, BT * (n - 1)).then_inc(passed, 1)
                    if col == 0:
                        dve.wait_ge(sc_ready, 3 * n + bank + 1).then_inc(passed, 1)
                    w = (i + 1) * P
                    dve.tensor_tensor_reduce(out=sm[h % 2][:, OFF[i]:OFF[i] + w], in0=sc[bank][:, col:col + w],
                                             in1=mask[:, SEQ - w:SEQ], scale=1.0, scalar=3e38, op0=ALU.add, op1=ALU.min,
                                             accum_out=low[h % 2][:, i:i + 1]).then_inc(mx_done, 1)

            def normalise(n, h):
                dve.wait_ge(ex_done, BT * n + BT)
                dve.reciprocal(inv[h % 2][:], tot[h % 2][:]).then_inc(inv_done, 1)
                dve.wait_ge(inv_done, n + 1)
                for i in range(BT):
                    a = pr[h % 2][:, OFF[i]:OFF[i] + (i + 1) * P]
                    dve.tensor_scalar(a, a, inv[h % 2][:, i:i + 1], None, ALU.mult).then_inc(nm_done, 1)

            def prob_rest(n, h, k):
                dve.wait_ge(hi_done, NF * n + k + 1)
                cols = slice(FCOL[k], FCOL[k] + FLEN[k])
                dve.tensor_tensor(ptl[h % 2][:, cols], pt[(NF * h + k) % 2][:, 0:FLEN[k]], pth[h % 2][:, cols].bitcast(F32),
                                  ALU.subtract).then_inc(lo_done, 1)

            def out_rest(n, h):
                dve.wait_ge(oh_done, n + 1)
                dve.tensor_tensor(ol[:, h, :], o_ps[:], oh[:, h, :].bitcast(F32), ALU.subtract).then_inc(ol_done, 1)

            def value_rest(s):
                dve.wait_ge(vh_done, s + 1)
                dve.tensor_tensor(vl[:].rearrange("p t d -> p (t d)"), pj[BANK[VT]][:],
                                  vh[:].rearrange("p t d -> p (t d)").bitcast(F32), ALU.subtract).then_inc(vl_done, 1)

            def add_output(s):
                for u in range(2):
                    dve.wait_ge(pj_ready, out_fill(s, u))
                    xb = x[:, bass.ds((s % BATCH) * BT + 2 * u, 2), :]
                    dve.tensor_tensor(xb, pj[OUT_BANK[u]][:].rearrange("p (t d) -> p t d", t=2), xb, ALU.add).then_inc(xu_done, 1)

            def step(s, first, last):
                for h in range(G):
                    n = G * s + h
                    h1, h2 = (h + 1) % G, (h + 2) % G
                    more1, more2 = not last or h + 1 < G, not last or h + 2 < G
                    if more2:
                        mask_min(n + 2, h2)
                    if more1:
                        prob_rest(n + 1, h1, 0)
                        prob_rest(n + 1, h1, 1)
                    if more2:
                        normalise(n + 2, h2)
                    if h == 0 and not first:
                        add_output(s - 1)
                    out_rest(n, h)
                    if h == G - 1 and not last:
                        value_rest(s + 1)
                    if more1:
                        prob_rest(n + 1, h1, 2)

            norm(0)
            z_rest(0)
            with dve.Fori(1, BATCH) as j:
                norm(j)
                z_rest(j)
            dve.wait_ge(const_in, 48)
            value_rest(0)
            mask_min(0, 0)
            normalise(0, 0)
            mask_min(1, 1)
            normalise(1, 1)
            for k in range(NF):
                prob_rest(0, 0, k)
            step(0, True, False)
            with dve.Fori(1, STEPS - 1) as s:
                step(s, False, False)
            step(STEPS - 1, False, True)
            add_output(STEPS - 1)

        @block.scalar
        def _(act):
            def z_lead(j):
                for c in range(C):
                    act.wait_ge(tz_done, C * j + c + 1)
                    act.activation(zh[:, c, bass.ds(j * SEQ, SEQ)], pj[c][:], ACT.Copy).then_inc(zhi_done, 1)

            def raw_out(s, r):
                if not (isinstance(s, int) and s == 0):
                    act.wait_ge(sum_done, NR * (s - 1) + r + 1)
                act.wait_ge(pj_ready, proj_fill(s, QFILL[r]))
                act.activation(raw[r][:], pj[BANK[QFILL[r]]][:], ACT.Copy).then_inc(raw_done, 1)

            def rotated_lead(s, r):
                act.wait_ge(sum_done, NR * s + r + 1)
                to = kh[:, bass.ds(s % 2, 1), :] if r == 0 else qh[:, r - 1:r, :]
                act.activation(to, rot[r % 2][:].unsqueeze(1), ACT.Copy).then_inc(qh_done, 1)

            def value_out(s):
                act.wait_ge(pj_ready, proj_fill(s, V))
                act.activation(vT[:], pj[BANK[V]][:], ACT.Copy).then_inc(vt_done, 1)

            def value_lead(s):
                act.wait_ge(pj_ready, proj_fill(s, VT))
                act.activation(vh[:].rearrange("p t d -> p (t d)"), pj[BANK[VT]][:], ACT.Copy).then_inc(vh_done, 1)

            def exps(n, h, tiles=QT):
                for i in tiles:
                    k = QT.index(i)
                    act.wait_ge(mx_done, BT * n + k + 1)
                    if k == 0 and not (isinstance(n, int) and n < 2):
                        act.wait_ge(pt_ready, NF * (n - 1))
                    cols = slice(OFF[i], OFF[i] + (i + 1) * P)
                    act.activation(pr[h % 2][:, cols], sm[h % 2][:, cols], ACT.Exp, bias=low[h % 2][:, i:i + 1],
                                   scale=-1.0, accum_out=tot[h % 2][:, i:i + 1]).then_inc(ex_done, 1)

            def prob_lead(n, h, k):
                act.wait_ge(pt_ready, NF * n + k + 1)
                cols = slice(FCOL[k], FCOL[k] + FLEN[k])
                act.activation(pth[h % 2][:, cols], pt[(NF * h + k) % 2][:, 0:FLEN[k]], ACT.Copy).then_inc(hi_done, 1)

            def out_lead(n, h):
                act.wait_ge(o_ready, n + 1)
                act.activation(oh[:, h, :], o_ps[:], ACT.Copy).then_inc(oh_done, 1)

            def step(s, last):
                for h in range(G):
                    n = G * s + h
                    h1, h2 = (h + 1) % G, (h + 2) % G
                    more1, more2 = not last or h + 1 < G, not last or h + 2 < G
                    if more2:
                        exps(n + 2, h2, QT[:1])
                    if more1:
                        prob_lead(n + 1, h1, 0)
                    if more2:
                        exps(n + 2, h2, QT[1:2])
                    if more1:
                        prob_lead(n + 1, h1, 1)
                    if more2:
                        exps(n + 2, h2, QT[2:])
                    if h == 0:
                        rotated_lead(s, 4)
                    if not last:
                        if h == 0:
                            raw_out(s + 1, 0)
                            raw_out(s + 1, 1)
                            rotated_lead(s + 1, 0)
                        else:
                            rotated_lead(s + 1, h)
                            raw_out(s + 1, h + 1)
                            if h == 1:
                                value_out(s + 1)
                    out_lead(n, h)
                    if h == G - 1 and not last:
                        value_lead(s + 1)
                    if more1:
                        prob_lead(n + 1, h1, 2)

            z_lead(0)
            with act.Fori(1, BATCH) as j:
                z_lead(j)
            for r in range(3):
                raw_out(0, r)
            value_out(0)
            raw_out(0, 3)
            value_lead(0)
            raw_out(0, 4)
            rotated_lead(0, 0)
            rotated_lead(0, 1)
            exps(0, 0)
            rotated_lead(0, 2)
            exps(1, 1)
            for k in range(NF):
                prob_lead(0, 0, k)
            rotated_lead(0, 3)
            step(0, False)
            with act.Fori(1, STEPS - 1) as s:
                step(s, False)
            step(STEPS - 1, True)

        @block.tensor
        def _(pe):
            def transpose_z(j):
                pe.wait_ge(z_done, BT * j + BT)
                if not isinstance(j, int):
                    pe.wait_ge(zlo_done, C * j)
                for c in range(C):
                    for t in range(BT):
                        r = pe.transpose(pj[c][:, t * P:(t + 1) * P], z[:, t, c * P:(c + 1) * P], ident[:])
                    r.then_inc(tz_done, 1)

            def project(s, fill, col):
                b = bass.ds((s % BATCH) * SEQ, SEQ)
                w = slice(col, col + HD)
                bank = pj[BANK[fill]][:]
                for c in range(C):
                    pe.matmul(bank, wqkv[0][:, c, w], zh[:, c, b], start=(c == 0), stop=False)
                    pe.matmul(bank, wqkv[0][:, c, w], zl[:, c, b], start=False, stop=False)
                    r = pe.matmul(bank, wqkv[1][:, c, w], zh[:, c, b], start=False, stop=(c == C - 1))
                r.then_inc(pj_ready, 1)

            def early(s):
                return isinstance(s, int) and s < 2

            def key(s):
                pe.wait_ge(wa_in, 32 * (s // BATCH) + 32)
                if not (isinstance(s, int) and s == 0):
                    pe.wait_ge(raw_done, NR * s)
                project(s, K, 0)

            def query(s, h):
                if h == 0:
                    if not (isinstance(s, int) and s == 0):
                        pe.wait_ge(vl_done, s)
                elif h == 1:
                    pe.wait_ge(wb_in, 32 * (s // BATCH) + 32)
                    if early(s):
                        pe.wait_ge(raw_done, NR * s + 1)
                    else:
                        pe.wait_ge(xu_done, 2 * (s - 2) + 1)
                else:
                    pe.wait_ge(raw_done, NR * s + h + 1)
                project(s, (Q0, Q1, Q2, Q3)[h], (h + 1) * HD)

            def value(s):
                if early(s):
                    pe.wait_ge(raw_done, NR * s + 2)
                else:
                    pe.wait_ge(xu_done, 2 * (s - 2) + 2)
                project(s, V, (G + 1) * HD)

            def value_T(s):
                pe.wait_ge(vt_done, s + 1)
                for t in range(BT):
                    r = pe.transpose(pj[BANK[VT]][:, t * P:(t + 1) * P], vT[:, t * P:(t + 1) * P], ident[:])
                r.then_inc(pj_ready, 1)

            def scores(n, s, h):
                pe.wait_ge(ql_done, NR * s + h + 2)
                key_row = bass.ds(s % 2, 1)
                for i in QT:
                    bank, col = PLACE[i]
                    if col == 0 and not (isinstance(n, int) and n == 0):
                        pe.wait_ge(mx_done, BT * (n - 1) + (1, 3, 4)[bank])
                    w = (i + 1) * P
                    o, q = sc[bank][:, col:col + w], slice(i * P, (i + 1) * P)
                    k_hi, k_lo = (k[:, key_row, 0:w].rearrange("p o k -> p (o k)") for k in (kh, kl))
                    pe.matmul(o, qh[:, h, q], k_hi, start=True, stop=False)
                    pe.matmul(o, qh[:, h, q], k_lo, start=False, stop=False)
                    r = pe.matmul(o, ql[:, h, q], k_hi, start=False, stop=True)
                    if i != 2:
                        r.then_inc(sc_ready, 1)

            def transpose_p(n, h, fills):
                for k in fills:
                    if k == 0:
                        pe.wait_ge(nm_done, BT * n + BT)
                    pe.wait_ge(lo_done, NF * n + k + 1)
                    for kt, col, _ in FILL[k]:
                        for i in range(kt, BT):
                            r = pe.transpose(pt[(NF * h + k) % 2][:, col + (i - kt) * P:col + (i - kt + 1) * P],
                                             pr[h % 2][:, OFF[i] + kt * P:OFF[i] + (kt + 1) * P], ident[:])
                    r.then_inc(pt_ready, 1)

            def weigh(n, s, h):
                pe.wait_ge(ol_done, n + 1)
                if h == 0:
                    pe.wait_ge(vl_done, s + 1)
                for k in range(NF):
                    pe.wait_ge(lo_done, LO0 + NF * n + k + 1)
                    for kt, col, w in FILL[k]:
                        o = o_ps[:, kt * P:SEQ]
                        a = slice(FCOL[k] + col, FCOL[k] + col + w)
                        end = k == NF - 1
                        pe.matmul(o, vh[:, kt, :], pth[h % 2][:, a], start=(kt == 0), stop=False)
                        pe.matmul(o, vh[:, kt, :], ptl[h % 2][:, a], start=False, stop=False)
                        r = pe.matmul(o, vl[:, kt, :], pth[h % 2][:, a], start=False, stop=end)
                r.then_inc(o_ready, 1)

            def output(s, projected):
                pe.wait_ge(wo_in, 32 * (s // BATCH) + 32)
                pe.wait_ge(ol_done, OL0 + G * s + G)
                for u in range(2):
                    if projected:
                        pe.wait_ge(raw_done, NR * (s + 2) + u + 1)
                    elif isinstance(s, int) and s == STEPS - 1:
                        pe.wait_ge(xu_done, 2 * (s - 1) + u + 1)
                    for t in range(2):
                        tok = slice((2 * u + t) * P, (2 * u + t + 1) * P)
                        o = pj[OUT_BANK[u]][:, t * D:(t + 1) * D]
                        for h in range(G):
                            pe.matmul(o, oh[:, h, tok], wo[0][:, h, :], start=(h == 0), stop=False)
                            pe.matmul(o, oh[:, h, tok], wo[1][:, h, :], start=False, stop=False)
                            r = pe.matmul(o, ol[:, h, tok], wo[0][:, h, :], start=False, stop=(h == G - 1))
                    r.then_inc(pj_ready, 1)

            def step(s, first, last):
                for h in range(G):
                    n = G * s + h
                    h1, h2 = (h + 1) % G, (h + 2) % G
                    more1, more2 = not last or h + 1 < G, not last or h + 2 < G
                    if more2:
                        scores(n + 2, s if h + 2 < G else s + 1, h2)
                    if more1:
                        transpose_p(n + 1, h1, (0, 1))
                    if h == 0:
                        if not last:
                            key(s + 1)
                            query(s + 1, 0)
                        if not first:
                            output(s - 1, not last)
                    elif not last:
                        query(s + 1, h)
                        if h == 1:
                            value(s + 1)
                        if h == 2:
                            value_T(s + 1)
                    weigh(n, s, h)
                    if more1:
                        transpose_p(n + 1, h1, (2,))

            transpose_z(0)
            with pe.Fori(1, BATCH) as j:
                transpose_z(j)
            pe.wait_ge(zlo_done, C * BATCH)
            key(0)
            query(0, 0)
            query(0, 1)
            value(0)
            query(0, 2)
            value_T(0)
            query(0, 3)
            scores(0, 0, 0)
            scores(1, 0, 1)
            transpose_p(0, 0, range(NF))
            step(0, True, False)
            with pe.Fori(1, STEPS - 1) as s:
                step(s, False, False)
            step(STEPS - 1, False, True)
            output(STEPS - 1, False)


def macaron_kernel(nc, d, out):
    with ExitStack() as ctx:
        x = ctx.enter_context(nc.sbuf_tensor("x", [P, TILES, D], F32))
        ident = ctx.enter_context(nc.sbuf_tensor("ident", [P, P], F32))
        split = nc.dram_tensor("attn_split", [KV, 2, P, GW], F32, kind="Internal").ap()
        ffn_phase(nc, "f1", d, x, ident, True, split, None)
        attention_phase(nc, d, x, ident, split)
        ffn_phase(nc, "f2", d, x, ident, False, None, out)


def shape_constants():
    half = HD // 2
    freq = (1.0 / np.float32(ROPE_BASE) ** (np.arange(half, dtype=np.float32) / np.float32(half))).astype(np.float32)
    ang = np.arange(SEQ, dtype=np.float32)[None, :] * freq[:, None]
    cos, sin = np.cos(ang).astype(np.float32), np.sin(ang).astype(np.float32)
    mask = np.zeros((P, SEQ), np.float32)
    mask[:, SEQ - P:] = np.triu(np.full((P, P), BIG, np.float32), 1)
    pick = np.zeros((2 * E, E, P), np.float32)
    for e in range(E):
        pick[e, e] = pick[E + e, e] = 1.0
    return {
        "ident": np.eye(P, dtype=np.float32),
        "iota": np.arange(E, dtype=np.float32),
        "mask": mask,
        "pick": pick.reshape(2 * E, E * P),
        "rope_cos": np.concatenate([cos, cos]),
        "rope_sin": np.concatenate([-sin, sin]),
    }


def kernel(**inputs):
    import concourse.bacc as _bacc
    from concourse.bass_utils import run_bass_kernel_spmd as _run

    a = {k: np.asarray(v) for k, v in inputs.items()}
    wq, wk, wv, wo = (a[f"L0_attn_{n}"] for n in ("wq", "wk", "wv", "wo"))
    groups = []
    for g in range(KV):
        rows = np.concatenate([wk[g * HD:(g + 1) * HD], wq[g * G * HD:(g + 1) * G * HD], wv[g * HD:(g + 1) * HD]])
        qkv = rows.T.reshape(C, P, QKV).transpose(1, 0, 2).reshape(P, C * QKV)
        og = wo[:, g * G * HD:(g + 1) * G * HD].T.reshape(G, HD, D).transpose(1, 0, 2).reshape(P, G * D)
        groups.append(np.concatenate([qkv, og], axis=1))
    arrays = {
        "x": a["L0_attn_x"].reshape(TOKENS, D),
        "attn_w": np.stack(groups),
        "key_weights": a["L0_attn_key_weights"],
        "router_w": a["L0_ffn_router_w"].reshape(C, P, E).transpose(1, 0, 2),
        "router_b": a["L0_ffn_router_b"],
        "expert_w": a["L0_ffn_expert_w"].reshape(E, C, P, D).transpose(0, 2, 1, 3).reshape(E, P, C * D),
        "expert_b": a["L0_ffn_expert_b"].reshape(E * C, P).T,
        "proj_w": a["L0_ffn_proj_w"].reshape(C, P, D).transpose(1, 0, 2),
        "proj_b": a["L0_ffn_proj_b"],
        "norm_w": a["L0_ffn_norm_w"],
        **shape_constants(),
    }
    arrays = {k: np.ascontiguousarray(v) for k, v in arrays.items()}
    nc = _bacc.Bacc("TRN2", target_bir_lowering=False, num_devices=1)
    d = {k: nc.dram_tensor(f"in_{k}", v.shape, mybir.dt.from_np(v.dtype), kind="ExternalInput").ap() for k, v in arrays.items()}
    out = nc.dram_tensor("out_x", (TOKENS, D), F32, kind="ExternalOutput").ap()
    macaron_kernel(nc, d, out)
    r = _run(nc, [{f"in_{k}": v for k, v in arrays.items()}], core_ids=[0])
    return r.results[0]["out_x"].reshape(a["L0_attn_x"].shape)
```

```python
from contextlib import ExitStack

import numpy as np

import concourse.bass as bass
from concourse import mybir

F32 = mybir.dt.float32
F32R = mybir.dt.float32r
U32 = mybir.dt.uint32
ALU = mybir.AluOpType
ACT = mybir.ActivationFunctionType

P = 128
D = 256
C = D // P
BATCH, SEQ = 4, 512
TOKENS = BATCH * SEQ
TILES = TOKENS // P
BT = SEQ // P
HEADS, KV, HD = 16, 4, 128
G = HEADS // KV
NR = G + 1
E = 8
LN_EPS = 1e-5
RMS_EPS = 1e-6
QKV = (G + 2) * HD
GW = C * QKV + G * D
COLS = C * E + C * D + E * C
ROWS = 2 * D + 2 * E + HEADS
BIG = 1e30
ROPE_BASE = 10000.0


def step_buffers(ga, gb, gc):
    half = C * (QKV - 2 * HD)
    wb = [gb[:, n * half:(n + 1) * half].rearrange("p (c n) -> p c n", c=C) for n in range(2)]
    raw = [ga[:, r * SEQ:(r + 1) * SEQ] for r in range(NR)]
    swap = [gc[:, r * SEQ:(r + 1) * SEQ].bitcast(F32) for r in range(NR)]
    return wb, raw, swap


def first_expert(gb):
    return gb[:, 2 * SEQ:2 * SEQ + C * D], gb[:, 2 * SEQ + C * D:2 * SEQ + 2 * C * D]


def ffn_phase(nc, tag, d, shared, step_sems, passed, first, split, out):
    x, ident, z, zh, zl, e_raw, wa_hi, wa_lo, cosT, sinT, ga, gb, gc, vT = shared
    raw_done, vt_done, wb_in, swap_in = step_sems
    with ExitStack() as ctx:
        def sb(name, shape, dt=F32):
            return ctx.enter_context(nc.sbuf_tensor(f"{tag}_{name}", shape, dt))

        def ps(name, shape):
            return ctx.enter_context(nc.psum_tensor(f"{tag}_{name}", shape, F32))

        def sem(name):
            return ctx.enter_context(nc.semaphore(f"{tag}_{name}"))

        e_hi, e_lo = sb("e_hi", [P, E, C * D], F32R), sb("e_lo", [P, E, C * D], F32R)
        parts = [(e_hi[:, e, :], e_lo[:, e, :]) for e in range(E)]
        if not first:
            parts[0] = first_expert(gb)
        cols = sb("cols", [P, COLS])
        r_raw = cols[:, 0:C * E].rearrange("p (c e) -> p c e", c=C)
        p_raw = cols[:, C * E:C * E + C * D].rearrange("p (c d) -> p c d", c=C)
        e_bias = cols[:, C * E + C * D:COLS]
        p_hi, p_lo = sb("p_hi", [P, C, D], F32R), sb("p_lo", [P, C, D], F32R)
        r_hl = sb("r_hl", [P, C, P], F32R)
        r_h0 = sb("r_h0", [P, C, P], F32R)
        rows = sb("rows", [P, ROWS])
        p_bias, n_w, r_bias = rows[:, 0:D], rows[:, D:2 * D], rows[:, 2 * D:2 * D + E]
        iota, kw = rows[:, 2 * D + E:2 * D + 2 * E], rows[:, 2 * D + 2 * E:ROWS]
        pick = sb("pick", [2 * E, E, P], F32R)
        st, mv, ve, rs = sb("st", [P, BT, 6]), sb("mv", [P, BT, 2]), sb("ve", [P, BT]), sb("rs", [P, BT])
        mhalf, warm = sb("mhalf", [P, BT]), sb("warm", [P, 3, BT])
        zres = sb("zres", [P, 2 * BT, D])
        rT = sb("rT", [2 * E, SEQ])
        l0, lg = sb("l0", [P, BT, E]), sb("lg", [P, BT, E])
        top, topi = sb("top", [P, BT, 8]), sb("topi", [P, BT, 8], U32)
        topf = sb("topf", [P, BT, 2])
        gap, th = sb("gap", [P, BT]), sb("th", [P, BT])
        w0, w1 = sb("w0", [P, BT]), sb("w1", [P, BT])
        oh0, oh1 = sb("oh0", [P, BT, E]), sb("oh1", [P, BT, E])
        full = sb("full", [P, BT, E])
        full_hi = sb("full_hi", [P, BT, E], F32R)
        fw = sb("fw", [P, BT, P])
        wT = sb("wT", [2 * E, SEQ], F32R)
        s_ring = [sb(f"s{n}", [P, SEQ]) for n in range(4)]
        u_ring = [sb(f"u{n}", [P, SEQ]) for n in range(4)]
        acc = sb("acc", [P, C, SEQ])
        ch, cl = sb("ch", [P, C, SEQ], F32R), sb("cl", [P, C, SEQ], F32R)
        y, sq = sb("y", [P, BT, D]), sb("sq", [P, BT, D])
        pick_raw = sq[0:2 * E].rearrange("p t d -> p (t d)").rearrange("p (e q) -> p e q", e=E)
        last5 = sq[:].rearrange("p (c t) d -> p c (t d)", c=C)
        ch_last, cl_last = e_hi[:, 0:C, :], e_lo[:, 0:C, :]
        ss, ms, rr = sb("ss", [P, BT]), sb("ms", [P, BT]), sb("rr", [P, BT])
        if first:
            a_raw, a_hi, a_lo = ga, gb, gc
            wb, raw, swap = step_buffers(ga, gb, gc)

        ex_ps = [ps(f"ex{n}", [P, SEQ]) for n in range(4)]
        w_ps = [ps(f"wide{n}", [P, SEQ]) for n in range(2)]
        t_ps = [ps(f"t{n}", [P, SEQ]) for n in range(2)]

        rows_in, cols_in, pick_in, pick_done = (sem(n) for n in ("rows_in", "cols_in", "pick_in", "pick_done"))
        e_hi_done, e_lo_done, p_split, r_split, setup, consts = (sem(n) for n in ("e_hi_done", "e_lo_done", "p_split", "r_split", "setup", "consts"))
        ln_stats, ln_aggr, ln_var, rstd_done, z_done = (sem(n) for n in ("ln_stats", "ln_aggr", "ln_var", "rstd_done", "z_done"))
        half_set = sem("half_set")
        tz_done, zhi_done, zlo_done, zres_done = (sem(n) for n in ("tz_done", "zhi_done", "zlo_done", "zres_done"))
        rout_done, rT_done, tb_done, gate, tanh_done = (sem(n) for n in ("rout_done", "rT_done", "tb_done", "gate", "tanh_done"))
        gap_done, fw_done, tw_done, wT_done = (sem(n) for n in ("gap_done", "fw_done", "tw_done", "wT_done"))
        ex_done, silu_done, sel_done, mult_done, pair_done, acc_done = (sem(n) for n in ("ex_done", "silu_done", "sel_done", "mult_done", "pair_done", "acc_done"))
        chi_done, clo_done, y_done, yadd_done, sq_done = (sem(n) for n in ("chi_done", "clo_done", "y_done", "yadd_done", "sq_done"))
        rms, rr_done, xn_done, x_done = (sem(n) for n in ("rms", "rr_done", "xn_done", "x_done"))
        if out is not None:
            out_done = sem("out_done")
        if first:
            e_in = [sem(f"e_in{n}") for n in range(E)]
            ident_in, x_in = sem("ident_in"), [sem(f"x_in{n}") for n in range(BATCH)]
            a_in, a_scaled, a_hi_done, a_lo_done, a_out, wa_in = (sem(n) for n in ("a_in", "a_scaled", "a_hi_done", "a_lo_done", "a_out", "wa_in"))
            tables_in = sem("tables_in")

        step_ps = t_ps + w_ps + w_ps
        RING = len(ex_ps)
        SILU0 = RING
        MULT0 = len(s_ring)
        X0 = 1
        SUMS = (1, 2, 3, 5, 7)
        ACC = C * len(SUMS)
        PAIRS = C * 2
        GATE = 20
        LAST = BATCH - 1
        J0 = 0 if first else 1

        def block_of(j):
            return j - BATCH if isinstance(j, int) and j >= BATCH else j

        block = ctx.enter_context(nc.Block())

        @block.sync
        def _(sp):
            xr = d["x"].rearrange("(b t p) d -> b p t d", t=BT, p=P)

            def load_group(i):
                sp.dma_start(a_raw[:], d["attn_w"][bass.ds(i, 1)].rearrange("o p n -> (o p) n")).then_inc(a_in, 16)

            def store_group(i, more):
                sp.wait_ge(a_lo_done, C * i + C).then_inc(passed, 1)
                if more:
                    load_group(i + 1)
                sp.dma_start(split[bass.ds(i, 1), 0].rearrange("o p n -> (o p) n"), a_hi[:].bitcast(F32)).then_inc(a_out, 16)
                sp.dma_start(split[bass.ds(i, 1), 1].rearrange("o p n -> (o p) n"), a_lo[:].bitcast(F32)).then_inc(a_out, 16)

            def store_block(i):
                sp.wait_ge(x_done, X0 + i + 1).then_inc(passed, 1)
                sp.dma_start(out.rearrange("(b t p) d -> b p t d", t=BT, p=P)[bass.ds(i, 1)].rearrange("o p t d -> (o p) t d"),
                             x[:, bass.ds(i * BT, BT), :]).then_inc(out_done, 16)

            if first:
                sp.dma_start(x[:, 0:BT, :], xr[0]).then_inc(x_in[0], 16)
                sp.dma_start(ident[:], d["ident"]).then_inc(ident_in, 16)
            sp.dma_start(cols[:], d["cols"]).then_inc(cols_in, 16)
            for e in range(E):
                if first:
                    sp.dma_start(e_raw[:, e, :], d["expert_w"][e]).then_inc(e_in[e], 16)
                if e == 1:
                    sp.dma_start(rows[:], d["rows"].partition_broadcast(P)).then_inc(rows_in, 16)
                    sp.dma_start(pick_raw, d["pick"]).then_inc(pick_in, 16)
                if first and e == 3:
                    sp.dma_start(x[:, BT:2 * BT, :], xr[1]).then_inc(x_in[1], 16)
            if first:
                load_group(0)
                for b in range(2, BATCH):
                    sp.dma_start(x[:, b * BT:(b + 1) * BT, :], xr[b]).then_inc(x_in[b], 16)
                sp.dma_start(cosT[:], d["rope_cos"]).then_inc(tables_in, 16)
                sp.dma_start(sinT[:], d["rope_sin"]).then_inc(tables_in, 16)
                with sp.Fori(0, KV - 1) as i:
                    store_group(i, True)
                sp.wait_ge(a_out, 32)
                for n, wa in enumerate((wa_hi, wa_lo)):
                    src = split[0, n, :, 0:C * QKV].rearrange("p (c n) -> p c n", c=C)
                    sp.dma_start(wa[:].bitcast(F32), src[:, :, 0:2 * HD]).then_inc(wa_in, 16)
                store_group(KV - 1, False)
                sp.wait_ge(a_out, 32 * KV)
                for n in range(2):
                    src = split[0, n, :, 0:C * QKV].rearrange("p (c n) -> p c n", c=C)
                    sp.dma_start(wb[n].bitcast(F32), src[:, :, 2 * HD:QKV]).then_inc(wb_in, 16)
                for r in range(NR):
                    sp.wait_ge(raw_done, r + 1)
                    sp.dma_start(swap[r][0:HD // 2, :], raw[r][HD // 2:HD, :]).then_inc(swap_in[r], 16)
                    sp.dma_start(swap[r][HD // 2:HD, :], raw[r][0:HD // 2, :]).then_inc(swap_in[r], 16)
                sp.wait_ge(tables_in, 32)
            if out is not None:
                with sp.Fori(0, LAST) as i:
                    store_block(i)
                for u in range(2):
                    rows_u = slice(LAST * BT + 2 * u, LAST * BT + 2 * u + 2)
                    sp.wait_ge(x_done, X0 + LAST + u + 1)
                    sp.dma_start(out.rearrange("(t p) d -> p t d", p=P)[:, rows_u, :], x[:, rows_u, :]).then_inc(out_done, 16)
                sp.wait_ge(out_done, 16 * (LAST + 2))

        @block.gpsimd
        def _(pool):
            pool.sem_inc(x_done, X0)
            pool.memset(mhalf[:], -0.5).then_inc(half_set, 1)
            pool.memset(warm[:, 0], 1.0).then_inc(half_set, 1)
            pool.wait_ge(half_set, 2)
            pool.tensor_tensor(warm[:, 1], warm[:, 0], mhalf[:], ALU.pow).then_inc(half_set, 1)

            def rstd(j):
                pool.wait_ge(ln_var, j - J0 + 1)
                pool.tensor_tensor(rs[:], ve[:], mhalf[:], ALU.pow).then_inc(rstd_done, 1)

            def residual(j):
                if first or not (isinstance(j, int) and j == 0):
                    pool.wait_ge(z_done, BT * (j - J0) + BT)
                pool.tensor_tensor(zres[:, bass.ds((j % 2) * BT, BT), :], z[:],
                                   p_bias.unsqueeze(1).to_broadcast([P, BT, D]), ALU.add).then_inc(zres_done, 1)

            def scale_queries(i):
                pool.wait_ge(consts, 2)
                pool.wait_ge(a_in, 16 * i + 16)
                for c in range(C):
                    q = a_raw[:, c * QKV + HD:c * QKV + QKV - HD].rearrange("p (h d) -> p h d", h=G)
                    pool.tensor_tensor(q, q, kw[:, bass.ds(i * G, G)].unsqueeze(2).to_broadcast([P, G, HD]),
                                       ALU.mult).then_inc(a_scaled, 1)

            def inverse_rms(i):
                pool.wait_ge(rms, i + 1)
                pool.tensor_tensor(rr[:], ms[:], mhalf[:], ALU.pow).then_inc(rr_done, 1)

            def add_rows(i):
                pool.wait_ge(xn_done, BT * i + BT)
                xb = x[:, bass.ds(i * BT, BT), :]
                pool.tensor_tensor(xb, xb, y[:], ALU.add).then_inc(x_done, 1)

            def body(i, prev, more):
                if more or first:
                    rstd(i + 1)
                if prev:
                    inverse_rms(i - 1)
                if first:
                    scale_queries(i)
                for j, e in enumerate(SUMS if more else SUMS[:2]):
                    for f in range(C):
                        n = C * e + f
                        if e < 4:
                            pool.wait_ge(mult_done, MULT0 + C * E * i + n + 1)
                        else:
                            pool.wait_ge(pair_done, PAIRS * i + C * (e // 2 - 2) + f + 1)
                        if j > 0:
                            pool.wait_ge(acc_done, ACC * i + C * (j - 1) + f + 1)
                        pool.tensor_tensor(acc[:, f, :], acc[:, f, :], u_ring[n % 4][:], ALU.add).then_inc(acc_done, 1)
                    if e == 3:
                        residual(i + 1)
                        if prev:
                            add_rows(i - 1)
                if not more:
                    for f in range(C):
                        e3, e4 = (u_ring[(C * e + f) % 4] for e in (3, 4))
                        pool.wait_ge(mult_done, MULT0 + C * E * i + C * 4 + f + 1)
                        pool.tensor_tensor(e4[:], e4[:], e3[:], ALU.add).then_inc(acc_done, 1)
                    for f in range(C):
                        e4 = u_ring[(C * 4 + f) % 4]
                        pool.wait_ge(mult_done, MULT0 + C * E * i + C * 5 + f + 1)
                        pool.wait_ge(acc_done, ACC * i + C * 2 + f + 1)
                        pool.tensor_tensor(e4[:], e4[:], last5[:, f, :], ALU.add).then_inc(acc_done, 1)
                    add_rows(i - 1)

            if first:
                rstd(0)
            pool.wait_ge(rows_in, 16)
            residual(0)
            body(0, False, True)
            with pool.Fori(1, LAST) as i:
                body(i, True, True)
            body(LAST, True, False)
            if first:
                rstd(BATCH + 1)
            for u in range(2):
                pool.wait_ge(rms, LAST + u + 1)
                pool.tensor_tensor(rr[:, 2 * u:2 * u + 2], ms[:, 2 * u:2 * u + 2], mhalf[:, 0:2], ALU.pow).then_inc(rr_done, 1)

        @block.vector
        def _(dve):
            dve.sem_inc(mult_done, MULT0)

            def norm_stats(j):
                b, k = block_of(j), (j - J0) * BT
                if isinstance(j, int) and j >= BATCH:
                    dve.wait_ge(x_done, X0 + b + 1)
                for t in range(BT):
                    dve.bn_stats(st[:, t, :], x[:, bass.ds(b * BT + t, 1), :]).then_inc(ln_stats, 1)
                dve.wait_ge(ln_stats, k + BT).then_inc(passed, 1)
                for t in range(BT):
                    dve.bn_aggr(mv[:, t, :], st[:, t, :]).then_inc(ln_aggr, 1)
                dve.wait_ge(ln_aggr, k + BT)
                dve.tensor_scalar(ve[:], mv[:, :, 1], LN_EPS, None, ALU.add).then_inc(ln_var, 1)

            def norm_rows(j):
                b = block_of(j)
                dve.wait_ge(rstd_done, j - J0 + 1)
                if isinstance(j, int) and j > BATCH:
                    dve.wait_ge(tz_done, C * j)
                elif not isinstance(j, int) or j > 0:
                    dve.wait_ge(zres_done, j)
                for t in range(BT):
                    dve.tensor_scalar(z[:, t, :], x[:, bass.ds(b * BT + t, 1), :], mv[:, t, 0:1], rs[:, t:t + 1],
                                      ALU.subtract, ALU.mult).then_inc(z_done, 1)

            def z_rest(j):
                for c in range(C):
                    dve.wait_ge(zhi_done, C * (j - J0) + c + 1)
                    to = bass.ds(block_of(j) * SEQ, SEQ)
                    dve.tensor_tensor(zl[:, c, to], t_ps[c][:], zh[:, c, to].bitcast(F32), ALU.subtract).then_inc(zlo_done, 1)

            def gating(j):
                g = GATE * j
                lp = t_ps[1][:, 0:BT * 2 * E].rearrange("p (t k) -> p t k", t=BT)
                dve.wait_ge(tb_done, j + 1)
                dve.tensor_tensor(l0[:], lp[:, :, E:2 * E], r_bias.unsqueeze(1).to_broadcast([P, BT, E]),
                                  ALU.add).then_inc(gate, 1)
                dve.wait_ge(gate, g + 1)
                dve.tensor_tensor(lg[:], lp[:, :, 0:E], l0[:], ALU.add).then_inc(gate, 1)
                dve.wait_ge(gate, g + 2).then_inc(passed, 1)
                for t in range(BT):
                    dve.max(top[:, t, :], lg[:, t, :]).then_inc(gate, 1)
                dve.wait_ge(gate, g + 6)
                dve.tensor_tensor(gap[:].unsqueeze(2), top[:, :, 0:1], top[:, :, 1:2], ALU.subtract).then_inc(gap_done, 1)
                for t in range(BT):
                    dve.max_index(topi[:, t, :], top[:, t, :], lg[:, t, :]).then_inc(gate, 1)
                dve.wait_ge(gate, g + 10)
                dve.tensor_copy(topf[:], topi[:, :, 0:2]).then_inc(gate, 1)
                dve.wait_ge(gate, g + 11)
                io = iota.unsqueeze(1).to_broadcast([P, BT, E])
                dve.tensor_tensor(oh0[:], io, topf[:, :, 0:1].to_broadcast([P, BT, E]), ALU.is_equal).then_inc(gate, 1)
                dve.tensor_tensor(oh1[:], io, topf[:, :, 1:2].to_broadcast([P, BT, E]), ALU.is_equal).then_inc(gate, 1)
                dve.wait_ge(tanh_done, j + 1)
                dve.tensor_scalar(w0[:], th[:], 0.5, 0.5, ALU.mult, ALU.add).then_inc(gate, 1)
                dve.tensor_scalar(w1[:], th[:], -0.5, 0.5, ALU.mult, ALU.add).then_inc(gate, 1)
                dve.wait_ge(gate, g + 15)
                dve.tensor_tensor(oh0[:], oh0[:], w0[:].unsqueeze(2).to_broadcast([P, BT, E]), ALU.mult).then_inc(gate, 1)
                dve.tensor_tensor(oh1[:], oh1[:], w1[:].unsqueeze(2).to_broadcast([P, BT, E]), ALU.mult).then_inc(gate, 1)
                dve.wait_ge(gate, g + 17)
                dve.tensor_tensor(full[:], oh0[:], oh1[:], ALU.add).then_inc(gate, 1)
                dve.wait_ge(gate, g + 18)
                dve.tensor_copy(full_hi[:], full[:]).then_inc(gate, 1)
                dve.wait_ge(gate, g + 19)
                dve.tensor_copy(fw[:, :, 0:E], full_hi[:].bitcast(F32)).then_inc(gate, 1)
                dve.tensor_tensor(fw[:, :, E:2 * E], full[:], full_hi[:].bitcast(F32), ALU.subtract).then_inc(fw_done, 1)

            def expert_rest(e):
                dve.wait_ge(e_hi_done, e + 1)
                hi, lo = parts[e]
                dve.tensor_tensor(lo, e_raw[:, e, :], hi.bitcast(F32), ALU.subtract).then_inc(e_lo_done, 1)

            def sum_rest(i):
                for f in range(C):
                    dve.wait_ge(chi_done, C * i + f + 1)
                    dve.tensor_tensor(cl[:, f, :], acc[:, f, :], ch[:, f, :].bitcast(F32), ALU.subtract).then_inc(clo_done, 1)

            def add_sixth(f):
                e6, e7 = s_ring[(C * 6 + f) % 4], s_ring[(C * 7 + f) % 4]
                dve.wait_ge(mult_done, MULT0 + C * E * LAST + C * 7 + f + 1)
                dve.tensor_tensor(e7[:], e7[:], e6[:], ALU.add).then_inc(pair_done, 1)

            def add_middle(f):
                e7 = s_ring[(C * 7 + f) % 4]
                dve.wait_ge(pair_done, PAIRS * LAST + 2 * f + 1)
                dve.wait_ge(acc_done, ACC * LAST + C * 3 + f + 1)
                dve.tensor_tensor(e7[:], e7[:], u_ring[(C * 4 + f) % 4][:], ALU.add).then_inc(pair_done, 1)

            def last_rest():
                for f in range(C):
                    dve.wait_ge(chi_done, C * BATCH + f + 1)
                    dve.tensor_tensor(cl_last[:, f, :], s_ring[(C * 7 + f) % 4][:], ch_last[:, f, :].bitcast(F32),
                                      ALU.subtract).then_inc(clo_done, 1)

            def add_last_residual(t):
                if t == 0:
                    dve.wait_ge(x_done, X0 + LAST)
                    dve.wait_ge(zres_done, BATCH)
                dve.wait_ge(y_done, 2 * LAST + t + 1)
                dve.tensor_tensor(y[:, t, :], ex_ps[t][:, 0:D], zres[:, (LAST % 2) * BT + t, :], ALU.add).then_inc(yadd_done, 1)

            def add_residual(i, u):
                if u == 0:
                    dve.wait_ge(x_done, X0 + i)
                    dve.wait_ge(zres_done, i + 1)
                dve.wait_ge(y_done, 2 * i + u + 1)
                dve.tensor_tensor(y[:, 2 * u:2 * u + 2, :], w_ps[u][:].rearrange("p (t d) -> p t d", t=2),
                                  zres[:, bass.ds((i % 2) * BT + 2 * u, 2), :], ALU.add).then_inc(yadd_done, 1)

            def mean_square(i):
                dve.wait_ge(sq_done, BT * i + BT)
                dve.tensor_scalar(ms[:], ss[:], 1.0 / D, RMS_EPS, ALU.mult, ALU.add).then_inc(rms, 1)

            def scale_rows(i):
                dve.wait_ge(rr_done, i + 1)
                for t in range(BT):
                    dve.scalar_tensor_tensor(out=y[:, t, :], in0=y[:, t, :], scalar=rr[:, t:t + 1], in1=n_w,
                                             op0=ALU.mult, op1=ALU.mult).then_inc(xn_done, 1)

            def group_rest(i, half):
                part = slice(half * GW // 2, (half + 1) * GW // 2)
                dve.wait_ge(a_hi_done, 2 * i + half + 1)
                dve.tensor_tensor(a_lo[:, part], a_raw[:, part], a_hi[:, part].bitcast(F32), ALU.subtract).then_inc(a_lo_done, 1)

            def body(i, prev, more):
                if not prev:
                    norm_stats(i + 1)
                gating(i)
                if prev:
                    sum_rest(i - 1)
                    if more or first:
                        norm_stats(i + 1)
                    add_residual(i - 1, 0)
                    add_residual(i - 1, 1)
                else:
                    norm_rows(i + 1)
                    expert_rest(4)
                    expert_rest(5)
                group_at = (3, 6) if more else (2, 3)
                for e in range(E):
                    for f in range(C):
                        n = C * e + f
                        dve.wait_ge(silu_done, SILU0 + C * E * i + n + 1)
                        if f == 0:
                            dve.wait_ge(sel_done, E * i + e + 1)
                        if e in (3, 4) or more and e in (5, 7):
                            dve.wait_ge(acc_done, ACC * i + C * (3 if e == 7 else e - 3) + f + 1)
                        if more and e == 6:
                            dve.wait_ge(pair_done, PAIRS * i + f + 1)
                        to = acc[:, f, :] if e == 0 else u_ring[n % 4][:]
                        if not more and e >= 5:
                            to = last5[:, f, :] if e == 5 else s_ring[n % 4][:]
                        dve.tensor_tensor(to, s_ring[n % 4][:], w_ps[e % 2][:], ALU.mult).then_inc(mult_done, 1)
                        if not more and e == E - 1:
                            if f > 0:
                                add_middle(f - 1)
                            add_sixth(f)
                    if e == 0 and prev:
                        mean_square(i - 1)
                    if e == 0 and prev and (more or first):
                        norm_rows(i + 1)
                    if e == 0 and not prev:
                        expert_rest(6)
                        expert_rest(7)
                        dve.wait_ge(e_hi_done, E + 1)
                        dve.tensor_tensor(p_lo[:], p_raw, p_hi[:].bitcast(F32), ALU.subtract).then_inc(p_split, 1)
                    if e == 2 and prev:
                        scale_rows(i - 1)
                    if e == 4 and (more or first):
                        z_rest(i + 1)
                    if e == 4 and not more:
                        sum_rest(i)
                    if more and e in (5, 7):
                        dve.wait_ge(mult_done, MULT0 + C * E * i + C * e + C)
                        for f in range(C):
                            even, odd = u_ring[(C * (e - 1) + f) % 4], u_ring[(C * e + f) % 4]
                            dve.tensor_tensor(odd[:], odd[:], even[:], ALU.add).then_inc(pair_done, 1)
                    if first and e in group_at:
                        group_rest(i, group_at.index(e))
                if not more:
                    add_middle(C - 1)

            if not first:
                dve.sem_inc(e_lo_done, 1)
            dve.memset(fw[:], 0.0).then_inc(setup, 1)
            dve.memset(r_hl[:].bitcast(F32), 0.0).then_inc(setup, 1)
            dve.memset(r_h0[:].bitcast(F32), 0.0).then_inc(setup, 1)
            if first:
                dve.wait_ge(x_in[0], 16)
                norm_stats(0)
            dve.wait_ge(cols_in, 16)
            dve.wait_ge(setup, 3)
            dve.tensor_copy(r_hl[:, :, 0:E], r_raw).then_inc(r_split, 1)
            dve.tensor_copy(r_h0[:, :, 0:E], r_raw).then_inc(r_split, 1)
            dve.wait_ge(r_split, 2)
            dve.tensor_tensor(r_hl[:, :, E:2 * E], r_raw, r_hl[:, :, 0:E].bitcast(F32), ALU.subtract).then_inc(r_split, 1)
            if first:
                norm_rows(0)
                z_rest(0)
            for e in range(0 if first else 1, E // 2):
                expert_rest(e)
            dve.wait_ge(pick_in, 16)
            dve.tensor_copy(pick[:], pick_raw).then_inc(pick_done, 1)
            dve.wait_ge(rows_in, 16)
            dve.tensor_scalar(n_w, n_w, 0.5, None, ALU.mult).then_inc(consts, 1)
            if first:
                dve.tensor_scalar(kw, kw, -float(HD) ** -0.5, None, ALU.mult).then_inc(consts, 1)
                dve.wait_ge(x_in[1], 16)
            body(0, False, True)
            if first:
                for b in range(2, BATCH):
                    dve.wait_ge(x_in[b], 16)
            with dve.Fori(1, LAST) as i:
                body(i, True, True)
            body(LAST, True, False)
            last_rest()
            if first:
                norm_stats(BATCH + 1)
            add_last_residual(0)
            add_last_residual(1)
            if first:
                norm_rows(BATCH + 1)
            add_last_residual(2)
            add_last_residual(3)
            for u in range(2):
                half = slice(2 * u, 2 * u + 2)
                dve.wait_ge(sq_done, BT * LAST + 2 * u + 2)
                dve.tensor_scalar(ms[:, half], ss[:, half], 1.0 / D, RMS_EPS, ALU.mult, ALU.add).then_inc(rms, 1)
            if first:
                z_rest(BATCH + 1)
            for u in range(2):
                dve.wait_ge(rr_done, LAST + u + 1)
                for t in (2 * u, 2 * u + 1):
                    dve.scalar_tensor_tensor(out=y[:, t, :], in0=y[:, t, :], scalar=rr[:, t:t + 1], in1=n_w,
                                             op0=ALU.mult, op1=ALU.mult).then_inc(xn_done, 1)
                dve.wait_ge(xn_done, BT * LAST + 2 * u + 2)
                xb = x[:, LAST * BT + 2 * u:LAST * BT + 2 * u + 2, :]
                dve.tensor_tensor(xb, xb, y[:, 2 * u:2 * u + 2, :], ALU.add).then_inc(x_done, 1)

        @block.scalar
        def _(act):
            act.sem_inc(silu_done, SILU0)

            def z_lead(j):
                for c in range(C):
                    act.wait_ge(tz_done, C * (j - J0) + c + 1)
                    act.activation(zh[:, c, bass.ds(block_of(j) * SEQ, SEQ)], t_ps[c][:], ACT.Copy).then_inc(zhi_done, 1)

            def logits_out(j):
                act.wait_ge(rout_done, j + 1)
                act.activation(rT[:], t_ps[0][0:2 * E, :], ACT.Copy).then_inc(rT_done, 1)

            def half_tanh(j):
                act.wait_ge(gap_done, j + 1)
                act.activation(th[:], gap[:], ACT.Tanh, scale=0.5).then_inc(tanh_done, 1)

            def weights_out(j):
                act.wait_ge(tw_done, j + 1)
                act.activation(wT[:], t_ps[0][0:2 * E, :], ACT.Copy).then_inc(wT_done, 1)

            def expert_lead(e):
                if first:
                    act.wait_ge(e_in[e], 16)
                act.activation(parts[e][0], e_raw[:, e, :], ACT.Copy).then_inc(e_hi_done, 1)

            def silu(i, e, chunks=range(C)):
                for f in chunks:
                    n = C * e + f
                    act.wait_ge(ex_done, C * E * i + n + 1)
                    act.wait_ge(mult_done, C * E * i + n + 1)
                    act.activation(s_ring[n % 4][:], ex_ps[n % RING][:], ACT.Silu,
                                   bias=e_bias[:, n:n + 1]).then_inc(silu_done, 1)

            def sum_lead(i):
                for f in range(C):
                    act.wait_ge(acc_done, ACC * i + (C if isinstance(i, int) and i == LAST else ACC - C) + f + 1)
                    act.activation(ch[:, f, :], acc[:, f, :], ACT.Copy).then_inc(chi_done, 1)

            def last_lead():
                for f in range(C):
                    act.wait_ge(pair_done, PAIRS * LAST + 2 * f + 2)
                    act.activation(ch_last[:, f, :], s_ring[(C * 7 + f) % 4][:], ACT.Copy).then_inc(chi_done, 1)

            def squares(i):
                for t in range(BT):
                    act.wait_ge(yadd_done, 2 * i + (t if isinstance(i, int) and i == LAST else t // 2) + 1)
                    act.activation(sq[:, t, :], y[:, t, :], ACT.Square, accum_out=ss[:, t:t + 1]).then_inc(sq_done, 1)

            def group_lead(i, half):
                if half == 0:
                    act.wait_ge(a_scaled, C * i + C)
                    if not (isinstance(i, int) and i == 0):
                        act.wait_ge(a_out, 32 * i)
                part = slice(half * GW // 2, (half + 1) * GW // 2)
                act.activation(a_hi[:, part], a_raw[:, part], ACT.Copy).then_inc(a_hi_done, 1)

            def step_out(k):
                act.wait_ge(ex_done, C * E * BATCH + k + 1)
                if k < NR:
                    if k == 0:
                        act.wait_ge(a_lo_done, C * KV)
                    act.activation(raw[k], step_ps[k][:], ACT.Copy).then_inc(raw_done, 1)
                else:
                    act.activation(vT[:], step_ps[k][:], ACT.Copy).then_inc(vt_done, 1)

            def body(i, prev, more):
                if first or prev:
                    logits_out(i)
                silu(i, 0)
                if not (first or prev):
                    logits_out(i)
                silu(i, 1, (0,))
                if prev:
                    silu(i, 1, (1,))
                    half_tanh(i)
                    sum_lead(i - 1)
                    weights_out(i)
                    squares(i - 1)
                else:
                    half_tanh(i)
                    silu(i, 1, (1,))
                    expert_lead(4)
                    expert_lead(5)
                    weights_out(i)
                    expert_lead(6)
                    expert_lead(7)
                    act.activation(p_hi[:], p_raw, ACT.Copy).then_inc(e_hi_done, 1)
                group_at = (3, 5) if more else (2, 3)
                for e in range(2, E):
                    silu(i, e)
                    if e == 4 and (more or first):
                        z_lead(i + 1)
                    if e == 5 and not more:
                        sum_lead(i)
                    if first and e in group_at:
                        group_lead(i, group_at.index(e))

            if not first:
                act.sem_inc(e_hi_done, 1)
            act.wait_ge(half_set, 2)
            act.activation(warm[:, 2], warm[:, 0], ACT.Silu).then_inc(half_set, 1)
            if first:
                z_lead(0)
            for e in range(0 if first else 1, E // 2):
                expert_lead(e)
            act.wait_ge(cols_in, 16)
            body(0, False, True)
            with act.Fori(1, LAST) as i:
                body(i, True, True)
            body(LAST, True, False)
            last_lead()
            if first:
                step_out(0)
                step_out(1)
            squares(LAST)
            if first:
                step_out(2)
                step_out(3)
                z_lead(BATCH + 1)
                step_out(4)
                step_out(5)

        @block.tensor
        def _(pe):
            def transpose_z(j):
                pe.wait_ge(z_done, BT * (j - J0) + BT)
                if isinstance(j, int) and j > BATCH:
                    pe.wait_ge(zlo_done, C * j)
                for c in range(C):
                    for t in range(BT):
                        r = pe.transpose(t_ps[c][:, t * P:(t + 1) * P], z[:, t, c * P:(c + 1) * P], ident[:])
                    r.then_inc(tz_done, 1)

            def transpose_first_z():
                for t in range(BT):
                    pe.wait_ge(z_done, t + 1)
                    for c in range(C):
                        r = pe.transpose(t_ps[c][:, t * P:(t + 1) * P], z[:, t, c * P:(c + 1) * P], ident[:])
                        if t == BT - 1:
                            r.then_inc(tz_done, 1)

            def router(j):
                if first or not (isinstance(j, int) and j == 0):
                    pe.wait_ge(zlo_done, C * (j - J0) + C)
                b = bass.ds(j * SEQ, SEQ)
                for c in range(C):
                    pe.matmul(t_ps[0][:], r_hl[:, c, :], zh[:, c, b], start=(c == 0), stop=False)
                    r = pe.matmul(t_ps[0][:], r_h0[:, c, :], zl[:, c, b], start=False, stop=(c == C - 1))
                r.then_inc(rout_done, 1)

            def logits_back(j):
                pe.wait_ge(rT_done, j + 1).then_inc(passed, 1)
                for t in range(BT):
                    r = pe.transpose(t_ps[1][:, t * 2 * E:(t + 1) * 2 * E], rT[:, t * P:(t + 1) * P], ident[0:2 * E, 0:2 * E])
                r.then_inc(tb_done, 1)

            def weights_T(j):
                pe.wait_ge(fw_done, j + 1)
                for t in range(BT):
                    r = pe.transpose(t_ps[0][:, t * P:(t + 1) * P], fw[:, t, :], ident[:])
                r.then_inc(tw_done, 1)

            def expert(i, e, chunks=range(C)):
                hi, lo = parts[e]
                if isinstance(i, int) and i == 0 and (first or e > 0):
                    pe.wait_ge(e_lo_done, e + 1)
                for f in chunks:
                    n = C * e + f
                    pe.wait_ge(silu_done, C * E * i + n + 1)
                    bank = ex_ps[n % RING][:]
                    b = bass.ds(i * SEQ, SEQ)
                    for c in range(C):
                        w = slice(c * D + f * P, c * D + (f + 1) * P)
                        pe.matmul(bank, hi[:, w], zh[:, c, b], start=(c == 0), stop=False)
                        pe.matmul(bank, hi[:, w], zl[:, c, b], start=False, stop=False)
                        r = pe.matmul(bank, lo[:, w], zh[:, c, b], start=False, stop=(c == C - 1))
                    r.then_inc(ex_done, 1)

            def select(i, e, prev):
                if e == 0:
                    pe.wait_ge(wT_done, i + 1)
                if e < 2 and prev:
                    pe.wait_ge(yadd_done, 2 * (i - 1) + e + 1)
                if e >= 2:
                    pe.wait_ge(mult_done, MULT0 + C * E * i + C * (e - 1))
                pe.matmul(w_ps[e % 2][:], pick[:, e, :], wT[:], start=True, stop=True).then_inc(sel_done, 1)

            def project(i):
                pe.wait_ge(clo_done, C * i + C)
                for u in range(2):
                    for t in range(2):
                        tok = slice((2 * u + t) * P, (2 * u + t + 1) * P)
                        o = w_ps[u][:, t * D:(t + 1) * D]
                        for f in range(C):
                            pe.matmul(o, ch[:, f, tok], p_hi[:, f, :], start=(f == 0), stop=False)
                            pe.matmul(o, ch[:, f, tok], p_lo[:, f, :], start=False, stop=False)
                            r = pe.matmul(o, cl[:, f, tok], p_hi[:, f, :], start=False, stop=(f == C - 1))
                    r.then_inc(y_done, 1)

            def project_first():
                pe.wait_ge(clo_done, C * LAST + C)
                for t in range(BT):
                    pe.wait_ge(silu_done, C * E * BATCH + t + 1)
                    tok, o = slice(t * P, (t + 1) * P), ex_ps[t][:, 0:D]
                    for f in range(C):
                        pe.matmul(o, ch[:, f, tok], p_hi[:, f, :], start=(f == 0), stop=False)
                        pe.matmul(o, ch[:, f, tok], p_lo[:, f, :], start=False, stop=False)
                        pe.matmul(o, cl[:, f, tok], p_hi[:, f, :], start=False, stop=False)

            def project_rest():
                for f in range(C):
                    pe.wait_ge(clo_done, C * BATCH + f + 1)
                    for t in range(BT):
                        tok, o = slice(t * P, (t + 1) * P), ex_ps[t][:, 0:D]
                        pe.matmul(o, ch_last[:, f, tok], p_hi[:, f, :], start=False, stop=False)
                        pe.matmul(o, ch_last[:, f, tok], p_lo[:, f, :], start=False, stop=False)
                        r = pe.matmul(o, cl_last[:, f, tok], p_hi[:, f, :], start=False, stop=(f == C - 1))
                        if f == C - 1:
                            r.then_inc(y_done, 1)

            def step_project(k):
                if k == 2:
                    pe.wait_ge(mult_done, MULT0 + C * E * BATCH)
                if k >= 4:
                    pe.wait_ge(raw_done, k - 2 + 1)
                (hi, lo), w = ((wa_hi, wa_lo), k) if k < 2 else (wb, k - 2)
                w = slice(w * HD, (w + 1) * HD)
                for c in range(C):
                    pe.matmul(step_ps[k][:], hi[:, c, w], zh[:, c, 0:SEQ], start=(c == 0), stop=False)
                    pe.matmul(step_ps[k][:], hi[:, c, w], zl[:, c, 0:SEQ], start=False, stop=False)
                    r = pe.matmul(step_ps[k][:], lo[:, c, w], zh[:, c, 0:SEQ], start=False, stop=(c == C - 1))
                r.then_inc(ex_done, 1)

            def body(i, prev, more):
                if first or prev:
                    router(i)
                    expert(i, 0)
                    logits_back(i)
                    expert(i, 1)
                else:
                    expert(i, 0)
                    pe.wait_ge(r_split, 3)
                    router(i)
                    expert(i, 1)
                    logits_back(i)
                expert(i, 2)
                weights_T(i)
                if prev:
                    project(i - 1)
                else:
                    pe.wait_ge(pick_done, 1)
                select(i, 0, prev)
                expert(i, 3)
                select(i, 1, prev)
                select(i, 2, prev)
                expert(i, 4)
                if more or first:
                    transpose_z(i + 1)
                select(i, 3, prev)
                expert(i, 5)
                select(i, 4, prev)
                expert(i, 6)
                select(i, 5, prev)
                select(i, 6, prev)
                if more:
                    expert(i, 7)
                    select(i, 7, prev)
                else:
                    expert(i, 7, (0,))
                    select(i, 7, prev)
                    expert(i, 7, (1,))

            if first:
                pe.wait_ge(ident_in, 16)
                transpose_first_z()
                pe.wait_ge(r_split, 3)
            body(0, False, True)
            pe.wait_ge(p_split, 1)
            with pe.Fori(1, LAST) as i:
                body(i, True, True)
            body(LAST, True, False)
            project_first()
            if first:
                pe.wait_ge(wa_in, 32)
                pe.wait_ge(zlo_done, C * (BATCH + 1))
                step_project(0)
                step_project(1)
            project_rest()
            if first:
                pe.wait_ge(wb_in, 32)
                step_project(2)
                step_project(3)
                pe.wait_ge(raw_done, 2)
                transpose_z(BATCH + 1)
                step_project(4)
                step_project(5)


def attention_phase(nc, d, shared, step_sems, passed, split):
    x, ident, z, zh, zl, e_raw, wa_hi, wa_lo, cosT, sinT, ga, gb, gc, vT = shared
    raw_done, vt_done, wb_in, swap_in = step_sems
    wb, raw, swap = step_buffers(ga, gb, gc)
    with ExitStack() as ctx:
        def sb(name, shape, dt=F32):
            return ctx.enter_context(nc.sbuf_tensor(f"at_{name}", shape, dt))

        def ps(name, shape):
            return ctx.enter_context(nc.psum_tensor(f"at_{name}", shape, F32))

        def sem(name):
            return ctx.enter_context(nc.semaphore(f"at_{name}"))

        STEPS = KV * BATCH
        OFF = [P * (i * (i + 1) // 2) for i in range(BT)]
        TRI = OFF[-1] + BT * P
        QT = (3, 2, 0, 1)
        FILL = (((0, 0, 4 * P),), ((1, 0, 3 * P), (3, 3 * P, P)), ((2, 0, 2 * P),))
        NF = len(FILL)
        FCOL, FLEN = (0, SEQ, 2 * SEQ), (SEQ, SEQ, 2 * P)

        mask = sb("mask", [P, SEQ])
        st, mv, ve, rs = sb("st", [P, BT, 6]), sb("mv", [P, 3, BT, 2]), sb("ve", [P, 3, BT]), sb("rs", [P, 3, BT])
        mhalf, warm = sb("mhalf", [P, BT]), sb("warm", [P, BT])
        wa = (wa_hi, wa_lo)
        wo = [sb(f"wo{n}", [P, G, D], F32R) for n in range(2)]
        rot = [sb(f"rot{n}", [P, SEQ]) for n in range(2)]
        kh, kl = sb("kh", [P, 2, SEQ], F32R), sb("kl", [P, 2, SEQ], F32R)
        qh, ql = sb("qh", [P, G, SEQ], F32R), sb("ql", [P, G, SEQ], F32R)
        vh, vl = sb("vh", [P, BT, HD], F32R), sb("vl", [P, BT, HD], F32R)
        sm = [sb(f"sm{n}", [P, TRI]) for n in range(2)]
        pr = [sb(f"pr{n}", [P, TRI]) for n in range(2)]
        low, tot, inv = ([sb(f"{n}{k}", [P, BT]) for k in range(2)] for n in ("low", "tot", "inv"))
        pth = [sb(f"pth{n}", [P, TRI], F32R) for n in range(2)]
        ptl = [sb(f"ptl{n}", [P, TRI], F32R) for n in range(2)]
        oh, ol = sb("oh", [P, G, SEQ], F32R), sb("ol", [P, G, SEQ], F32R)

        def out_parts(s, h):
            if isinstance(s, int) and s == STEPS - 1 and h == 0:
                return gb[:, 0:SEQ], gb[:, SEQ:2 * SEQ]
            return oh[:, h, :], ol[:, h, :]

        pj = [ps(f"pj{n}", [P, SEQ]) for n in range(2)]
        sc = [ps(f"sc{n}", [P, SEQ]) for n in range(3)]
        pt = [ps(f"pt{n}", [P, SEQ]) for n in range(2)]
        o_ps = ps("o", [P, SEQ])
        PLACE = {3: (0, 0), 2: (1, 0), 0: (1, 3 * P), 1: (2, 0)}

        mask_in, wa_in, wo_in = (sem(n) for n in ("mask_in", "wa_in", "wo_in"))
        ln_stats, ln_aggr, ln_var, rstd_done, z_done = (sem(n) for n in ("ln_stats", "ln_aggr", "ln_var", "rstd_done", "z_done"))
        half_set = sem("half_set")
        tz_done, zhi_done, zlo_done = (sem(n) for n in ("tz_done", "zhi_done", "zlo_done"))
        pj_ready, sc_ready, pt_ready, o_ready = (sem(n) for n in ("pj_ready", "sc_ready", "pt_ready", "o_ready"))
        qh_done, vh_done, vl_done = (sem(n) for n in ("qh_done", "vh_done", "vl_done"))
        ex_done, hi_done, lo_done, oh_done, ol_done = (sem(n) for n in ("ex_done", "hi_done", "lo_done", "oh_done", "ol_done"))
        mx_done, inv_done, nm_done, xu_done = (sem(n) for n in ("mx_done", "inv_done", "nm_done", "xu_done"))
        sin_done, sum_done, ql_done, early = (sem(n) for n in ("sin_done", "sum_done", "ql_done", "early"))

        NORMS = ((0, BATCH - 2, pj), (1, BATCH - 1, pj), (2, 0, sc[:2]))
        EARLY = 3
        WA0 = 32
        LO0 = 2
        OL0 = 1
        K, Q0, V, Q1, VT, Q2, Q3 = range(7)
        BANK = {K: 0, Q0: 1, V: 0, Q1: 1, VT: 0, Q2: 1, Q3: 1}
        OUT_BANK = (1, 0)
        QFILL = (K, Q0, Q1, Q2, Q3)
        NEXT = (Q1, V, "W0", "W1", Q2, Q3, "K", "Q0", VT)
        BEFORE = 4
        FULL, BASE = len(NEXT), BEFORE + len(NEXT) - 3
        TAIL = BASE + FULL * (STEPS - 3)

        def proj_fill(t, k):
            if isinstance(t, int) and t == 0:
                return BEFORE - 1
            if k in (K, Q0):
                if isinstance(t, int) and t < 3:
                    return 1 + k if t == 1 else BEFORE + 4 + k
                return BASE + FULL * (t - 3) + 7 + k
            if isinstance(t, int) and t == 1:
                return BEFORE + [Q1, V, Q2, Q3, None, None, VT].index(k)
            if isinstance(t, int) and t == STEPS - 1 and k == VT:
                return TAIL + FULL - 2
            return BASE + FULL * (t - 2) + 1 + NEXT.index(k)

        def out_fill(s, u):
            if isinstance(s, int) and s >= STEPS - 2:
                return TAIL + FULL - 2 + 2 * (s - (STEPS - 2)) + u + 1
            return BASE + FULL * s + 3 + u

        block = ctx.enter_context(nc.Block())

        @block.sync
        def _(sp):
            def load_proj(g, to, cols, done):
                for n in range(2):
                    src = split[bass.ds(g, 1), n, :, 0:C * QKV].rearrange("o p (c n) -> (o p) c n", c=C)
                    sp.dma_start(to[n][:, :, :].bitcast(F32), src[:, :, cols]).then_inc(done, 16)

            def load_wo(g):
                for n in range(2):
                    sp.dma_start(wo[n][:].rearrange("p h n -> p (h n)").bitcast(F32),
                                 split[bass.ds(g, 1), n, :, C * QKV:GW].rearrange("o p n -> (o p) n")).then_inc(wo_in, 16)

            FIRST, LATER = slice(0, 2 * HD), slice(2 * HD, QKV)

            def swaps(s, new_wo=None, new_proj=None):
                for r in range(NR):
                    sp.wait_ge(raw_done, NR * s + r + 1).then_inc(passed, 1)
                    sp.dma_start(swap[r][0:HD // 2, :], raw[r][HD // 2:HD, :]).then_inc(swap_in[r], 16)
                    sp.dma_start(swap[r][HD // 2:HD, :], raw[r][0:HD // 2, :]).then_inc(swap_in[r], 16)
                    if r == 1 and new_proj is not None:
                        load_proj(new_proj, wa, FIRST, wa_in)
                    if r == 3 and new_wo is not None:
                        load_wo(new_wo)
                    if r == NR - 1 and new_proj is not None:
                        load_proj(new_proj, wb, LATER, wb_in)

            sp.dma_start(mask[:], d["mask"]).then_inc(mask_in, 16)
            load_wo(0)
            with sp.Fori(1, BATCH - 1) as s:
                swaps(s)
            swaps(BATCH - 1, new_proj=1)
            with sp.Fori(1, KV - 1) as g:
                swaps(BATCH * g)
                swaps(BATCH * g + 1, new_wo=g)
                swaps(BATCH * g + 2)
                swaps(BATCH * g + 3, new_proj=g + 1)
            last = BATCH * (KV - 1)
            swaps(last)
            swaps(last + 1, new_wo=KV - 1)
            with sp.Fori(last + 2, STEPS) as s:
                swaps(s)

        @block.gpsimd
        def _(pool):
            def rest(s, r):
                pool.wait_ge(qh_done, NR * s + r + 1)
                to, lead = ((kl, kh) if r == 0 else (ql, qh))
                k = bass.ds(s % 2, 1) if r == 0 else slice(r - 1, r)
                pool.tensor_tensor(to[:, k, :], rot[r % 2][:].unsqueeze(1), lead[:, k, :].bitcast(F32),
                                   ALU.subtract).then_inc(ql_done, 1)

            def rotate(s, r):
                if r >= 2:
                    pool.wait_ge(ql_done, NR * s + r - 1)
                elif not (isinstance(s, int) and s == 0):
                    pool.wait_ge(ql_done, NR * s)
                pool.wait_ge(raw_done, NR * s + r + 1)
                pool.tensor_tensor(rot[r % 2][:], raw[r], cosT[:], ALU.mult)
                pool.wait_ge(swap_in[r], 32 * s + 32)
                pool.tensor_tensor(swap[r], swap[r], sinT[:], ALU.mult).then_inc(sin_done, 1)
                pool.wait_ge(sin_done, NR * s + r + 1)
                if isinstance(s, int) and s == 0 and r in (1, EARLY):
                    pool.wait_ge(qh_done, r)
                pool.tensor_tensor(rot[r % 2][:], rot[r % 2][:], swap[r], ALU.add).then_inc(sum_done, 1)

            def rstd(k):
                pool.wait_ge(ln_var, k + 1)
                pool.tensor_tensor(rs[:, k], ve[:, k], mhalf[:], ALU.pow).then_inc(rstd_done, 1)

            def rope(s):
                rotate(s, 0)
                for r in range(1, NR):
                    rest(s, r - 1)
                    rotate(s, r)

            pool.memset(mhalf[:], -0.5).then_inc(half_set, 1)
            pool.wait_ge(half_set, 1)
            pool.sem_inc(sin_done, 1)
            rotate(0, 1)
            pool.sem_inc(sin_done, 1)
            rotate(0, EARLY)
            pool.wait_ge(ql_done, EARLY)
            for r in range(EARLY + 1, NR):
                rest(0, r - 1)
                rotate(0, r)
            rstd(0)
            rstd(1)
            with pool.Fori(1, STEPS) as s:
                rest(s - 1, NR - 1)
                rope(s)
            rest(STEPS - 1, NR - 1)
            rstd(2)

        @block.vector
        def _(dve):
            dve.sem_inc(wa_in, WA0)
            dve.sem_inc(lo_done, LO0)
            dve.sem_inc(ol_done, OL0)

            def norm_stats(k, b, _):
                if k == 2:
                    dve.wait_ge(xu_done, 2 * (STEPS - BATCH + b + 1))
                for t in range(BT):
                    dve.bn_stats(st[:, t, :], x[:, b * BT + t, :]).then_inc(ln_stats, 1)
                dve.wait_ge(ln_stats, k * BT + BT)
                for t in range(BT):
                    dve.bn_aggr(mv[:, k, t, :], st[:, t, :]).then_inc(ln_aggr, 1)
                dve.wait_ge(ln_aggr, k * BT + BT)
                dve.tensor_scalar(ve[:, k], mv[:, k, :, 1], LN_EPS, None, ALU.add).then_inc(ln_var, 1)

            def norm_rows(k, b, _):
                dve.wait_ge(rstd_done, k + 1)
                if k == 1:
                    dve.wait_ge(tz_done, C)
                for t in range(BT):
                    dve.tensor_scalar(z[:, t, :], x[:, b * BT + t, :], mv[:, k, t, 0:1], rs[:, k, t:t + 1],
                                      ALU.subtract, ALU.mult).then_inc(z_done, 1)

            def z_rest(k, b, banks):
                for c in range(C):
                    dve.wait_ge(zhi_done, C * k + c + 1)
                    to = slice(b * SEQ, (b + 1) * SEQ)
                    dve.tensor_tensor(zl[:, c, to], banks[c][:], zh[:, c, to].bitcast(F32), ALU.subtract).then_inc(zlo_done, 1)

            def mask_min(n, h):
                for k, i in enumerate(QT):
                    bank, col = PLACE[i]
                    if k == 0 and not (isinstance(n, int) and n < 2):
                        dve.wait_ge(ex_done, BT * (n - 1)).then_inc(passed, 1)
                    if col == 0:
                        dve.wait_ge(sc_ready, 3 * n + bank + 1).then_inc(passed, 1)
                    w = (i + 1) * P
                    dve.tensor_tensor_reduce(out=sm[h % 2][:, OFF[i]:OFF[i] + w], in0=sc[bank][:, col:col + w],
                                             in1=mask[:, SEQ - w:SEQ], scale=1.0, scalar=3e38, op0=ALU.add, op1=ALU.min,
                                             accum_out=low[h % 2][:, i:i + 1]).then_inc(mx_done, 1)

            def normalise(n, h):
                dve.wait_ge(ex_done, BT * n + BT)
                dve.reciprocal(inv[h % 2][:], tot[h % 2][:]).then_inc(inv_done, 1)
                dve.wait_ge(inv_done, n + 1)
                for i in range(BT):
                    a = pr[h % 2][:, OFF[i]:OFF[i] + (i + 1) * P]
                    dve.tensor_scalar(a, a, inv[h % 2][:, i:i + 1], None, ALU.mult).then_inc(nm_done, 1)

            def prob_rest(n, h, k):
                dve.wait_ge(hi_done, NF * n + k + 1)
                cols = slice(FCOL[k], FCOL[k] + FLEN[k])
                dve.tensor_tensor(ptl[h % 2][:, cols], pt[(NF * h + k) % 2][:, 0:FLEN[k]], pth[h % 2][:, cols].bitcast(F32),
                                  ALU.subtract).then_inc(lo_done, 1)

            def out_rest(n, s, h):
                lead, rest = out_parts(s, h)
                dve.wait_ge(oh_done, n + 1)
                dve.tensor_tensor(rest, o_ps[:], lead.bitcast(F32), ALU.subtract).then_inc(ol_done, 1)

            def value_rest(s):
                dve.wait_ge(vh_done, s + 1)
                dve.tensor_tensor(vl[:].rearrange("p t d -> p (t d)"), pj[BANK[VT]][:],
                                  vh[:].rearrange("p t d -> p (t d)").bitcast(F32), ALU.subtract).then_inc(vl_done, 1)

            def add_output(s, halves=(0, 1), part=0):
                for u in halves:
                    dve.wait_ge(pj_ready, out_fill(s, u) + 2 * part)
                    xb = x[:, bass.ds((s % BATCH) * BT + 2 * u, 2), :]
                    rows = pt[u] if part else pj[OUT_BANK[u]]
                    if part:
                        dve.wait_ge(xu_done, 2 * s + u + 1)
                    dve.tensor_tensor(xb, rows[:].rearrange("p (t d) -> p t d", t=2), xb, ALU.add).then_inc(xu_done, 1)

            def step(s, first, last):
                for h in range(G):
                    n = G * s + h
                    h1, h2 = (h + 1) % G, (h + 2) % G
                    more1, more2 = not last or h + 1 < G, not last or h + 2 < G
                    if more2:
                        mask_min(n + 2, h2)
                    if more1:
                        prob_rest(n + 1, h1, 0)
                        prob_rest(n + 1, h1, 1)
                    if first and h < 2:
                        norm_rows(*NORMS[h])
                    if last and h == 2:
                        norm_rows(*NORMS[2])
                    if more2:
                        normalise(n + 2, h2)
                    if h == 0 and not first:
                        add_output(s - 1, (0,) if last else (0, 1))
                    if h == G - 1 and last:
                        add_output(s, (0,))
                    out_rest(n, s, h)
                    if h == G - 1 and last:
                        add_output(s, (1,))
                    if last and h == 2:
                        hi, lo = first_expert(gb)
                        dve.wait_ge(early, 5)
                        dve.tensor_tensor(lo, e_raw[:, 0, :], hi.bitcast(F32), ALU.subtract).then_inc(early, 1)
                    if more1:
                        prob_rest(n + 1, h1, 2)
                    if h == G - 1 and not last:
                        value_rest(s + 1)
                    if first and h < 2:
                        z_rest(*NORMS[h])
                    if last and h == 1:
                        add_output(s - 1, (1,))
                    if last and h == 0:
                        norm_stats(*NORMS[2])
                    if last and h == 2:
                        z_rest(*NORMS[2])

            def early_cos(r):
                dve.wait_ge(raw_done, r + 1)
                dve.tensor_tensor(rot[r % 2][:], raw[r], cosT[:], ALU.mult).then_inc(early, 1)

            def early_sum(r):
                dve.wait_ge(swap_in[r], 32)
                dve.tensor_tensor(swap[r], swap[r], sinT[:], ALU.mult).then_inc(early, 1)
                dve.wait_ge(early, r + 2)
                dve.tensor_tensor(rot[r % 2][:], rot[r % 2][:], swap[r], ALU.add).then_inc(sum_done, 1)

            def early_rest(r):
                to, lead = (kl[:, 0, :], kh[:, 0, :]) if r == 0 else (ql[:, r - 1, :], qh[:, r - 1, :])
                dve.wait_ge(qh_done, r + 1)
                dve.tensor_tensor(to, rot[r % 2][:], lead.bitcast(F32), ALU.subtract).then_inc(ql_done, 1)

            early_cos(0)
            early_sum(0)
            early_rest(0)
            dve.wait_ge(ql_done, 1)
            early_cos(2)
            early_rest(1)
            early_sum(2)
            early_rest(2)
            dve.wait_ge(mask_in, 16)
            mask_min(0, 0)
            norm_stats(*NORMS[0])
            normalise(0, 0)
            mask_min(1, 1)
            prob_rest(0, 0, 0)
            prob_rest(0, 0, 1)
            norm_stats(*NORMS[1])
            normalise(1, 1)
            value_rest(0)
            prob_rest(0, 0, 2)
            step(0, True, False)
            with dve.Fori(1, STEPS - 1) as s:
                step(s, False, False)
            step(STEPS - 1, False, True)
            add_output(STEPS - 1, part=1)

        @block.scalar
        def _(act):
            def z_lead(k, b, banks):
                for c in range(C):
                    act.wait_ge(tz_done, C * k + c + 1)
                    act.activation(zh[:, c, b * SEQ:(b + 1) * SEQ], banks[c][:], ACT.Copy).then_inc(zhi_done, 1)

            def raw_out(s, r):
                if not (isinstance(s, int) and s == 0):
                    act.wait_ge(sum_done, NR * (s - 1) + r + 1)
                act.wait_ge(pj_ready, proj_fill(s, QFILL[r]))
                act.activation(raw[r], pj[BANK[QFILL[r]]][:], ACT.Copy).then_inc(raw_done, 1)

            def rotated_lead(s, r):
                act.wait_ge(sum_done, NR * s + r + 1)
                to = kh[:, bass.ds(s % 2, 1), :] if r == 0 else qh[:, r - 1:r, :]
                act.activation(to, rot[r % 2][:].unsqueeze(1), ACT.Copy).then_inc(qh_done, 1)

            def value_out(s):
                act.wait_ge(pj_ready, proj_fill(s, V))
                act.activation(vT[:], pj[BANK[V]][:], ACT.Copy).then_inc(vt_done, 1)

            def value_lead(s):
                act.wait_ge(pj_ready, proj_fill(s, VT))
                act.activation(vh[:].rearrange("p t d -> p (t d)"), pj[BANK[VT]][:], ACT.Copy).then_inc(vh_done, 1)

            def exps(n, h, tiles=QT):
                for i in tiles:
                    k = QT.index(i)
                    act.wait_ge(mx_done, BT * n + k + 1)
                    if k == 0 and not (isinstance(n, int) and n < 2):
                        act.wait_ge(pt_ready, NF * (n - 1))
                    cols = slice(OFF[i], OFF[i] + (i + 1) * P)
                    act.activation(pr[h % 2][:, cols], sm[h % 2][:, cols], ACT.Exp, bias=low[h % 2][:, i:i + 1],
                                   scale=-1.0, accum_out=tot[h % 2][:, i:i + 1]).then_inc(ex_done, 1)

            def prob_lead(n, h, k):
                act.wait_ge(pt_ready, NF * n + k + 1)
                cols = slice(FCOL[k], FCOL[k] + FLEN[k])
                act.activation(pth[h % 2][:, cols], pt[(NF * h + k) % 2][:, 0:FLEN[k]], ACT.Copy).then_inc(hi_done, 1)

            def out_lead(n, s, h):
                act.wait_ge(o_ready, n + 1)
                act.activation(out_parts(s, h)[0], o_ps[:], ACT.Copy).then_inc(oh_done, 1)

            def step(s, first, ahead):
                for h in range(G):
                    n = G * s + h
                    h1, h2 = (h + 1) % G, (h + 2) % G
                    more1, more2 = ahead or h + 1 < G, ahead or h + 2 < G
                    if more1:
                        prob_lead(n + 1, h1, 0)
                        prob_lead(n + 1, h1, 1)
                    if more2:
                        exps(n + 2, h2, QT[:2])
                    if h == 0 and ahead:
                        if not first:
                            raw_out(s + 1, 2)
                        value_out(s + 1)
                    if more2:
                        exps(n + 2, h2, QT[2:])
                    if h in (1, 2) and ahead:
                        raw_out(s + 1, h + 2)
                    if h == G - 1 and ahead == 2:
                        raw_out(s + 2, 0)
                        raw_out(s + 2, 1)
                    if h == 0 and ahead:
                        rotated_lead(s + 1, 0)
                    if h == 0 and ahead and not first:
                        rotated_lead(s + 1, 1)
                    out_lead(n, s, h)
                    if more1:
                        prob_lead(n + 1, h1, 2)
                    if h > 0 and ahead:
                        rotated_lead(s + 1, h + 1)
                    if h == G - 1 and ahead:
                        value_lead(s + 1)
                    if first and h < 2:
                        z_lead(*NORMS[h])
                    if first and h == 0:
                        rotated_lead(s + 1, 1)
                    if not ahead and h == 0:
                        act.activation(first_expert(gb)[0], e_raw[:, 0, :], ACT.Copy).then_inc(early, 1)
                    if not ahead and h == 2:
                        z_lead(*NORMS[2])

            act.wait_ge(half_set, 1)
            act.activation(warm[:], mhalf[:], ACT.Exp).then_inc(half_set, 1)
            rotated_lead(0, 0)
            rotated_lead(0, 1)
            raw_out(1, 0)
            raw_out(1, 1)
            rotated_lead(0, 2)
            rotated_lead(0, 3)
            exps(0, 0)
            value_lead(0)
            raw_out(1, 2)
            prob_lead(0, 0, 0)
            prob_lead(0, 0, 1)
            rotated_lead(0, 4)
            exps(1, 1)
            prob_lead(0, 0, 2)
            step(0, True, 2)
            with act.Fori(1, STEPS - 2) as s:
                step(s, False, 2)
            step(STEPS - 2, False, 1)
            step(STEPS - 1, False, 0)

        @block.tensor
        def _(pe):
            def transpose_z(k, b, banks):
                pe.wait_ge(z_done, BT * k + BT)
                if k == 0:
                    pe.wait_ge(vt_done, 2)
                if k < 2:
                    pe.wait_ge(raw_done, NR + 3 + k)
                if k == 2:
                    pe.wait_ge(mx_done, BT * G * STEPS)
                for c in range(C):
                    for t in range(BT):
                        r = pe.transpose(banks[c][:, t * P:(t + 1) * P], z[:, t, c * P:(c + 1) * P], ident[:])
                    r.then_inc(tz_done, 1)

            def project(s, fill, col):
                b = bass.ds((s % BATCH) * SEQ, SEQ)
                (hi, lo), col = (wa, col) if col < 2 * HD else (wb, col - 2 * HD)
                w = slice(col, col + HD)
                bank = pj[BANK[fill]][:]
                for c in range(C):
                    pe.matmul(bank, hi[:, c, w], zh[:, c, b], start=(c == 0), stop=False)
                    pe.matmul(bank, hi[:, c, w], zl[:, c, b], start=False, stop=False)
                    r = pe.matmul(bank, lo[:, c, w], zh[:, c, b], start=False, stop=(c == C - 1))
                r.then_inc(pj_ready, 1)

            def key(t):
                pe.wait_ge(wa_in, 32 * (t // BATCH) + WA0)
                if isinstance(t, int) and t == 2:
                    pe.wait_ge(vt_done, 2)
                elif not isinstance(t, int) or t > 2:
                    pe.wait_ge(xu_done, 2 * (t - 3) + 2)
                project(t, K, 0)

            def query(t, h):
                if h == 0 and not (isinstance(t, int) and t == 1):
                    pe.wait_ge(raw_done, NR * t)
                if h == 1:
                    pe.wait_ge(wb_in, 32 * (t // BATCH) + 32)
                if h == 2 and not (isinstance(t, int) and t < 2):
                    pe.wait_ge(xu_done, 2 * (t - 2) + 1)
                elif h > 0:
                    pe.wait_ge(raw_done, NR * t + h + 1)
                project(t, (Q0, Q1, Q2, Q3)[h], (h + 1) * HD)

            def value(t):
                pe.wait_ge(vl_done, t)
                project(t, V, (G + 1) * HD)

            def value_T(t, after_key):
                pe.wait_ge(vt_done, t + 1)
                if after_key:
                    pe.wait_ge(raw_done, NR * (t + 1) + 1)
                elif t > 0:
                    pe.wait_ge(xu_done, 2 * (t - 2) + 2)
                for k in range(BT):
                    r = pe.transpose(pj[BANK[VT]][:, k * P:(k + 1) * P], vT[:, k * P:(k + 1) * P], ident[:])
                r.then_inc(pj_ready, 1)

            def scores(n, s, h):
                pe.wait_ge(ql_done, NR * s + h + 2)
                key_row = bass.ds(s % 2, 1)
                for i in QT:
                    bank, col = PLACE[i]
                    if col == 0 and not (isinstance(n, int) and n == 0):
                        pe.wait_ge(mx_done, BT * (n - 1) + (1, 3, 4)[bank])
                    w = (i + 1) * P
                    o, q = sc[bank][:, col:col + w], slice(i * P, (i + 1) * P)
                    k_hi, k_lo = (k[:, key_row, 0:w].rearrange("p o k -> p (o k)") for k in (kh, kl))
                    pe.matmul(o, qh[:, h, q], k_hi, start=True, stop=False)
                    pe.matmul(o, qh[:, h, q], k_lo, start=False, stop=False)
                    r = pe.matmul(o, ql[:, h, q], k_hi, start=False, stop=True)
                    if i != 2:
                        r.then_inc(sc_ready, 1)

            def transpose_p(n, h, fills):
                for k in fills:
                    if k == 0:
                        pe.wait_ge(nm_done, BT * n + BT)
                    pe.wait_ge(lo_done, NF * n + k + 1)
                    for kt, col, _ in FILL[k]:
                        for i in range(kt, BT):
                            r = pe.transpose(pt[(NF * h + k) % 2][:, col + (i - kt) * P:col + (i - kt + 1) * P],
                                             pr[h % 2][:, OFF[i] + kt * P:OFF[i] + (kt + 1) * P], ident[:])
                    r.then_inc(pt_ready, 1)

            def weigh(n, s, h):
                pe.wait_ge(ol_done, n + 1)
                if h == 0:
                    pe.wait_ge(vl_done, s + 1)
                for k in range(NF):
                    pe.wait_ge(lo_done, LO0 + NF * n + k + 1)
                    for kt, col, w in FILL[k]:
                        o = o_ps[:, kt * P:SEQ]
                        a = slice(FCOL[k] + col, FCOL[k] + col + w)
                        end = k == NF - 1
                        pe.matmul(o, vh[:, kt, :], pth[h % 2][:, a], start=(kt == 0), stop=False)
                        pe.matmul(o, vh[:, kt, :], ptl[h % 2][:, a], start=False, stop=False)
                        r = pe.matmul(o, vl[:, kt, :], pth[h % 2][:, a], start=False, stop=end)
                r.then_inc(o_ready, 1)

            def output(s, heads=range(G), halves=(0, 1)):
                pe.wait_ge(wo_in, 32 * (s // BATCH) + 32)
                pe.wait_ge(ol_done, OL0 + G * s + heads[-1] + 1)
                for u in halves:
                    bank = pt[u] if heads[0] else pj[OUT_BANK[u]]
                    if heads[0]:
                        pe.wait_ge(lo_done, LO0 + NF * G * STEPS)
                    elif isinstance(s, int) and s == STEPS - 1:
                        pe.wait_ge(xu_done, 2 * (s - 1) + u + 1)
                    elif isinstance(s, int) and s == STEPS - 2:
                        if u == 0:
                            pe.wait_ge(raw_done, NR * STEPS)
                        else:
                            pe.wait_ge(vl_done, STEPS)
                    elif u == 0:
                        pe.wait_ge(raw_done, NR * (s + 2) + 3)
                    else:
                        pe.wait_ge(vt_done, s + 3)
                    for t in range(2):
                        tok = slice((2 * u + t) * P, (2 * u + t + 1) * P)
                        o = bank[:, t * D:(t + 1) * D]
                        for h in heads:
                            hi, lo = out_parts(s, h)
                            pe.matmul(o, hi[:, tok], wo[0][:, h, :], start=(h == heads[0]), stop=False)
                            pe.matmul(o, hi[:, tok], wo[1][:, h, :], start=False, stop=False)
                            r = pe.matmul(o, lo[:, tok], wo[0][:, h, :], start=False, stop=(h == heads[-1]))
                    r.then_inc(pj_ready, 1)

            def step(s, first, ahead):
                for h in range(G):
                    n = G * s + h
                    h1, h2 = (h + 1) % G, (h + 2) % G
                    more1, more2 = ahead or h + 1 < G, ahead or h + 2 < G
                    if more2:
                        scores(n + 2, s if h + 2 < G else s + 1, h2)
                    if more1:
                        transpose_p(n + 1, h1, (0, 1))
                    if h == 0:
                        if ahead and not first:
                            query(s + 1, 1)
                        if ahead:
                            value(s + 1)
                        if not first:
                            output(s - 1, halves=(0, 1) if ahead else (0,))
                    elif h == 1 and not ahead:
                        output(s - 1, halves=(1,))
                    elif h in (1, 2) and ahead:
                        if first:
                            pe.wait_ge(zlo_done, C * h)
                        query(s + 1, h + 1)
                    elif h == G - 1 and ahead == 2:
                        key(s + 2)
                        query(s + 2, 0)
                    elif h == G - 1 and not ahead:
                        output(s, range(G - 1), (0,))
                    weigh(n, s, h)
                    if h == G - 1 and not ahead:
                        output(s, range(G - 1), (1,))
                    if h == G - 1 and ahead:
                        value_T(s + 1, ahead == 2)
                    if more1:
                        transpose_p(n + 1, h1, (2,))
                    if first and h < 2:
                        transpose_z(*NORMS[h])
                    if not ahead and h == 2:
                        transpose_z(*NORMS[2])

            key(1)
            query(1, 0)
            scores(0, 0, 0)
            value_T(0, True)
            query(1, 1)
            scores(1, 0, 1)
            transpose_p(0, 0, range(NF))
            step(0, True, 2)
            with pe.Fori(1, STEPS - 2) as s:
                step(s, False, 2)
            step(STEPS - 2, False, 1)
            step(STEPS - 1, False, 0)
            output(STEPS - 1, range(G - 1, G))


def macaron_kernel(nc, d, out):
    with ExitStack() as ctx:
        shared = [ctx.enter_context(nc.sbuf_tensor(name, shape, dt)) for name, shape, dt in (
            ("x", [P, TILES, D], F32),
            ("ident", [P, P], F32),
            ("z", [P, BT, D], F32),
            ("zh", [P, C, TOKENS], F32R),
            ("zl", [P, C, TOKENS], F32R),
            ("e_raw", [P, E, C * D], F32),
            ("wa_hi", [P, C, 2 * HD], F32R),
            ("wa_lo", [P, C, 2 * HD], F32R),
            ("cos", [P, SEQ], F32),
            ("sin", [P, SEQ], F32),
            ("ga", [P, GW], F32),
            ("gb", [P, GW], F32R),
            ("gc", [P, GW], F32R),
            ("vT", [P, SEQ], F32))]
        step_sems = [ctx.enter_context(nc.semaphore(n)) for n in
                     ("raw_done", "vt_done", "wb_in", *(f"swap_in{r}" for r in range(G + 1)))]
        raw_done, vt_done, wb_in, *swap_in = step_sems
        step_sems = raw_done, vt_done, wb_in, swap_in
        passed = ctx.enter_context(nc.semaphore("passed"))
        split = nc.dram_tensor("attn_split", [KV, 2, P, GW], F32, kind="Internal").ap()
        ffn_phase(nc, "f1", d, shared, step_sems, passed, True, split, None)
        attention_phase(nc, d, shared, step_sems, passed, split)
        ffn_phase(nc, "f2", d, shared, step_sems, passed, False, None, out)


def shape_constants():
    half = HD // 2
    freq = (1.0 / np.float32(ROPE_BASE) ** (np.arange(half, dtype=np.float32) / np.float32(half))).astype(np.float32)
    ang = np.arange(SEQ, dtype=np.float32)[None, :] * freq[:, None]
    cos, sin = np.cos(ang).astype(np.float32), np.sin(ang).astype(np.float32)
    mask = np.zeros((P, SEQ), np.float32)
    mask[:, SEQ - P:] = np.triu(np.full((P, P), BIG, np.float32), 1)
    pick = np.zeros((2 * E, E, P), np.float32)
    for e in range(E):
        pick[e, e] = pick[E + e, e] = 1.0
    return {
        "ident": np.eye(P, dtype=np.float32),
        "mask": mask,
        "pick": pick,
        "rope_cos": np.concatenate([cos, cos]),
        "rope_sin": np.concatenate([-sin, sin]),
    }


def kernel(**inputs):
    import concourse.bacc as _bacc
    from concourse.bass_utils import run_bass_kernel_spmd as _run

    a = {k: np.asarray(v) for k, v in inputs.items()}
    wq, wk, wv, wo = (a[f"L0_attn_{n}"] for n in ("wq", "wk", "wv", "wo"))
    groups = []
    for g in range(KV):
        rows = np.concatenate([wk[g * HD:(g + 1) * HD], wq[g * G * HD:(g + 1) * G * HD], wv[g * HD:(g + 1) * HD]])
        qkv = rows.T.reshape(C, P, QKV).transpose(1, 0, 2).reshape(P, C * QKV)
        og = wo[:, g * G * HD:(g + 1) * G * HD].T.reshape(G, HD, D).transpose(1, 0, 2).reshape(P, G * D)
        groups.append(np.concatenate([qkv, og], axis=1))
    arrays = {
        "x": a["L0_attn_x"].reshape(TOKENS, D),
        "attn_w": np.stack(groups),
        "cols": np.concatenate([a["L0_ffn_router_w"].reshape(C, P, E).transpose(1, 0, 2).reshape(P, C * E),
                                a["L0_ffn_proj_w"].reshape(C, P, D).transpose(1, 0, 2).reshape(P, C * D),
                                a["L0_ffn_expert_b"].reshape(E * C, P).T], axis=1),
        "rows": np.concatenate([a["L0_ffn_proj_b"], a["L0_ffn_norm_w"], a["L0_ffn_router_b"],
                                np.arange(E, dtype=np.float32), a["L0_attn_key_weights"]]),
        "expert_w": a["L0_ffn_expert_w"].reshape(E, C, P, D).transpose(0, 2, 1, 3).reshape(E, P, C * D),
        **shape_constants(),
    }
    arrays = {k: np.ascontiguousarray(v) for k, v in arrays.items()}
    nc = _bacc.Bacc("TRN2", target_bir_lowering=False, num_devices=1)
    d = {k: nc.dram_tensor(f"in_{k}", v.shape, mybir.dt.from_np(v.dtype), kind="ExternalInput").ap() for k, v in arrays.items()}
    out = nc.dram_tensor("out_x", (TOKENS, D), F32, kind="ExternalOutput").ap()
    macaron_kernel(nc, d, out)
    r = _run(nc, [{f"in_{k}": v for k, v in arrays.items()}], core_ids=[0])
    return r.results[0]["out_x"].reshape(a["L0_attn_x"].shape)
```
